# Optimizing a Trainium2 kernel written in Bass

```python
import numpy as np
import jax
import jax.numpy as jnp

def _softmax(x, axis=-1):
    return jax.nn.softmax(x, axis=axis)

def _gelu(x):
    return jax.nn.gelu(x, approximate=True)

def _silu(x):
    return jax.nn.silu(x)

def _sigmoid(x):
    return jax.nn.sigmoid(x)

def _layernorm(x, axis=-1, eps=1e-05):
    m = jnp.mean(x, axis=axis, keepdims=True)
    v = jnp.var(x, axis=axis, keepdims=True)
    return (x - m) / jnp.sqrt(v + eps)

def _scatter_add(tgt, idx, src, axis=0):
    return tgt.at[idx].add(src)

def _segment_sum(src, seg, n):
    return jax.ops.segment_sum(src, seg, n)
kernel_name = 'mk_gnn_resnorm_d1_gnn_r8_c6e068'

def setup_inputs(seed: int=0):
    np.random.seed(seed)
    _w = jnp.asarray

    def _rec_inputs():
        import jax
        import jax.numpy as jnp
        _gk = jax.random.key(seed)
        x = -0.0002117 + 1 * jax.random.normal(jax.random.fold_in(_gk, 1), (6250, 512), jnp.float32)
        src = jax.random.randint(jax.random.fold_in(_gk, 2), (100000,), 0, 6250, jnp.int32)
        dst = jax.random.randint(jax.random.fold_in(_gk, 3), (100000,), 0, 6250, jnp.int32)
        _o = jnp.argsort(dst, stable=True)
        src = src[_o]
        dst = dst[_o]
        return (x, src, dst)
    x, src, dst = _rec_inputs()

    def _L0_gnn_setup():
        import jax, jax.numpy as jnp
        import numpy as np
        N, D = (6250, 512)
        E = 50000
        P_POW, M_SCALE, EPS = (2, 2, 1e-10)

        def _layer_norm(x, gamma, beta, eps=1e-05):
            mu = jnp.mean(x, axis=-1, keepdims=True)
            var = jnp.mean(jnp.square(x - mu), axis=-1, keepdims=True)
            return (x - mu) * jax.lax.rsqrt(var + eps) * gamma + beta

        def _former(Q, V):
            Q = jax.nn.relu(_layer_norm(Q, 1.0, 0.0))
            H = jnp.sum(Q, axis=1, keepdims=True) ** P_POW
            m = (jnp.max(H) - jnp.min(H)) * M_SCALE
            H = jnp.pi / (2.0 * m) * H
            cosQ = Q * jnp.cos(H)
            sinQ = Q * jnp.sin(H)
            out = cosQ @ (cosQ.T @ V) + sinQ @ (sinQ.T @ V)
            norm = cosQ @ jnp.sum(cosQ, axis=0)[:, None] + sinQ @ jnp.sum(sinQ, axis=0)[:, None] + EPS
            return out / norm

        def _gcn(x, edge_index, Wg, bg):
            loop = jnp.arange(N, dtype=edge_index.dtype)
            src = jnp.concatenate([edge_index[0], loop])
            dst = jnp.concatenate([edge_index[1], loop])
            deg = jax.ops.segment_sum(jnp.ones_like(src, dtype=x.dtype), dst, num_segments=N)
            dinv = jax.lax.rsqrt(jnp.maximum(deg, 1e-12))
            coef = (dinv[src] * dinv[dst])[:, None]
            xw = x @ Wg
            return jax.ops.segment_sum(xw[src] * coef, dst, num_segments=N) + bg
        key = jax.random.key(seed)
        ks = jax.random.split(key, 10)
        s = 1.0 / np.sqrt(D)
        return {'x': jax.random.normal(ks[0], (N, D), dtype=jnp.float32), 'edge_index': jax.random.randint(ks[1], (2, E), 0, N, dtype=jnp.int64), 'Wq': jax.random.uniform(ks[2], (D, D), jnp.float32, -s, s), 'bq': jax.random.uniform(ks[3], (D,), jnp.float32, -s, s), 'Wv': jax.random.uniform(ks[4], (D, D), jnp.float32, -s, s), 'bv': jax.random.uniform(ks[5], (D,), jnp.float32, -s, s), 'Wg': jax.random.uniform(ks[6], (D, D), jnp.float32, -s, s), 'bg': jax.random.uniform(ks[7], (D,), jnp.float32, -s, s), 'gamma': jnp.ones((D,), jnp.float32), 'beta': jnp.zeros((D,), jnp.float32)}
    _L0_gnn_all = _L0_gnn_setup()
    _L0_gnn_in = {k: v for k, v in _L0_gnn_all.items() if k in ('Wq', 'bq', 'Wv', 'bv', 'Wg', 'bg', 'gamma', 'beta')}
    del _L0_gnn_all
    return {'x': x, 'src': src, 'dst': dst, 'L0_gnn_Wq': _L0_gnn_in['Wq'], 'L0_gnn_bq': _L0_gnn_in['bq'], 'L0_gnn_Wv': _L0_gnn_in['Wv'], 'L0_gnn_bv': _L0_gnn_in['bv'], 'L0_gnn_Wg': _L0_gnn_in['Wg'], 'L0_gnn_bg': _L0_gnn_in['bg'], 'L0_gnn_gamma': _L0_gnn_in['gamma'], 'L0_gnn_beta': _L0_gnn_in['beta']}

def reference(x, src, dst, L0_gnn_Wq, L0_gnn_bq, L0_gnn_Wv, L0_gnn_bv, L0_gnn_Wg, L0_gnn_bg, L0_gnn_gamma, L0_gnn_beta):
    import jax
    import jax.numpy as jnp

    def _L0_gnn_ref(x, edge_index, Wq, bq, Wv, bv, Wg, bg, gamma, beta):
        import jax, jax.numpy as jnp
        import numpy as np
        N, D = (6250, 512)
        E = 50000
        P_POW, M_SCALE, EPS = (2, 2, 1e-10)

        def _layer_norm(x, gamma, beta, eps=1e-05):
            mu = jnp.mean(x, axis=-1, keepdims=True)
            var = jnp.mean(jnp.square(x - mu), axis=-1, keepdims=True)
            return (x - mu) * jax.lax.rsqrt(var + eps) * gamma + beta

        def _former(Q, V):
            Q = jax.nn.relu(_layer_norm(Q, 1.0, 0.0))
            H = jnp.sum(Q, axis=1, keepdims=True) ** P_POW
            m = (jnp.max(H) - jnp.min(H)) * M_SCALE
            H = jnp.pi / (2.0 * m) * H
            cosQ = Q * jnp.cos(H)
            sinQ = Q * jnp.sin(H)
            out = cosQ @ (cosQ.T @ V) + sinQ @ (sinQ.T @ V)
            norm = cosQ @ jnp.sum(cosQ, axis=0)[:, None] + sinQ @ jnp.sum(sinQ, axis=0)[:, None] + EPS
            return out / norm

        def _gcn(x, edge_index, Wg, bg):
            loop = jnp.arange(N, dtype=edge_index.dtype)
            src = jnp.concatenate([edge_index[0], loop])
            dst = jnp.concatenate([edge_index[1], loop])
            deg = jax.ops.segment_sum(jnp.ones_like(src, dtype=x.dtype), dst, num_segments=N)
            dinv = jax.lax.rsqrt(jnp.maximum(deg, 1e-12))
            coef = (dinv[src] * dinv[dst])[:, None]
            xw = x @ Wg
            return jax.ops.segment_sum(xw[src] * coef, dst, num_segments=N) + bg
        Q = jax.nn.relu(x @ Wq + bq)
        V = x @ Wv + bv
        out = _former(Q, V) + _gcn(x, edge_index, Wg, bg) + V
        out = _layer_norm(out, gamma, beta)
        out = jax.nn.relu(out)
        return out
    edge_index = jnp.stack([src, dst])
    x = _layernorm(x + _L0_gnn_ref(x, edge_index, L0_gnn_Wq, L0_gnn_bq, L0_gnn_Wv, L0_gnn_bv, L0_gnn_Wg, L0_gnn_bg, L0_gnn_gamma, L0_gnn_beta), axis=-1)
    return x

_drawn_inputs = setup_inputs


def setup_inputs(seed=0):
    import zlib

    import numpy as np

    out = dict(_drawn_inputs(seed))
    spreads = {'L0_gnn_gamma': (1.0, 0.2), 'L0_gnn_beta': (0.0, 0.1)}
    factors = {}
    for name, (base, spread) in spreads.items():
        noise = np.random.default_rng([zlib.crc32(name.encode()), seed]).standard_normal(out[name].shape)
        drawn = base * np.exp(spread * noise) if base else spread * noise
        out[name] = jnp.asarray(drawn.astype(out[name].dtype))
    for name, factor in factors.items():
        out[name] = (out[name] * factor).astype(out[name].dtype)
    return out
```

```python
import math
from contextlib import ExitStack

import concourse.bass as bass
from concourse import mybir

F32 = mybir.dt.float32
F32R = mybir.dt.float32r
BF16 = mybir.dt.bfloat16
I32 = mybir.dt.int32
ALU = mybir.AluOpType
ACT = mybir.ActivationFunctionType
AX = mybir.AxisListType
ENG = mybir.EngineType

P = 128
N = 6250
D = 512
E = 100000
EPS_LN = 1e-5
EPS_NORM = 1e-10
TILES = -(-N // P)
NPAD = TILES * P
KD = D // P
K = 2
UNITS = 2
L = UNITS * K * P
GROUPS = -(-E // L)
PHASE_STEPS = (3, 1, 1)
STEPS = TILES * sum(PHASE_STEPS)
assert STEPS >= GROUPS + TILES - 1
RING = 4
ROWBLOCKS = -(-(STEPS - TILES + 1) * UNITS * K // P)
CHUNKS = ROWBLOCKS * P
EPAD = CHUNKS * P
HB = 14
HBATCHES = -(-E // (P * HB))
TCOLS = -(-STEPS // P)
FAR = float(1 << 20)


def build(nc, x, src, dst, Wq, bq, Wv, bv, Wg, bg, gamma, beta, out):
    with ExitStack() as ctx:
        def sb(name, shape, dt):
            return ctx.enter_context(nc.sbuf_tensor("sb_" + name, shape, dt))

        def sem(name):
            return ctx.enter_context(nc.semaphore(name))

        y_dram = nc.dram_tensor("y_scratch", [NPAD, D], F32).ap()
        q_dram = nc.dram_tensor("q_scratch", [NPAD, D], F32).ap()
        v_dram = nc.dram_tensor("v_scratch", [NPAD, D], F32).ap()
        tab_dram = nc.dram_tensor("tab_scratch", [2, TCOLS * P], I32).ap()
        off_dram = nc.dram_tensor("off_scratch", [1, TCOLS * P], F32).ap()

        def rows(a):
            return a.rearrange("(t p) d -> p t d", p=P)

        x_r, y_r, q_r, v_r, out_r = rows(x), rows(y_dram), rows(q_dram), rows(v_dram), rows(out)

        acc = sb("acc", [P, TILES, D], F32)
        edges = sb("edges", [P, CHUNKS, 2], I32)
        w_split = sb("w_split", [P, 2, 2, KD, D], F32R)
        r_pool = sb("r_pool", [P, 8192], F32R)
        f_pool = sb("f_pool", [P, 7168], F32)
        ident = sb("ident", [P, P], F32)
        iota_row = sb("iota_row", [P, P], F32)
        tables = sb("tables", [P, max(3 * STEPS, 2 * D)], I32)
        tab = tables[0:1, 0:2 * STEPS].rearrange("p (w s) -> p w s", w=2)
        off_t = tables[:, 2 * STEPS:3 * STEPS].bitcast(F32)
        stage = sb("stage", [P, RING, K, 2], I32)
        var_q = sb("var_q", [P, 64], F32)
        s0 = sb("s0", [P, TILES], F32)
        dinv = sb("dinv", [P, TILES], F32)
        rstd = sb("rstd", [P, TILES], F32)
        cs = sb("cs", [P, TILES, 4], F32)
        cs_split = sb("cs_split", [P, TILES, 2, 2], F32R)
        qn = sb("qn", [P, KD, 4], F32R)
        small = sb("small", [P, 64], F32)
        bank = [ctx.enter_context(nc.psum_tensor(f"bank{b}", [P, D], F32)) for b in range(8)]
        agg_bank = bank[6:8]

        g_hl = r_pool[:, 0:4096].rearrange("p (s h f) -> p s h f", s=2, h=2)
        x_hl = r_pool[:, 4096:6144].rearrange("p (s h d) -> p s h d", s=2, h=2)
        biases = r_pool[:, 6144:7168].rearrange("p (w d) -> p w d", w=2)
        ones_row = r_pool[:, 7168:7296]
        onehot = r_pool[:, 7296:7296 + 2 * K * P].rearrange("p (s k n) -> p s k n", s=2, k=K)
        qv_hl = w_split[:, 1, :, :, :].rearrange("p h c d -> p (h c d)").rearrange(
            "p (s w h d) -> p s w h d", s=2, w=2, h=2)
        wg_hl = r_pool[:, 0:4096].rearrange("p (h c d) -> p h c d", h=2, c=KD)
        qz_hl = r_pool[:, 4096:8192].rearrange("p (s w h d) -> p s w h d", s=2, w=2, h=2)
        gath = f_pool[:, 0:4096].rearrange("p (s f) -> p s f", s=RING)
        x_in = f_pool[:, 4096:5120].rearrange("p (s d) -> p s d", s=2)
        q_out = f_pool[:, 5120:6144].rearrange("p (s d) -> p s d", s=2)
        v_out = f_pool[:, 6144:7168].rearrange("p (s d) -> p s d", s=2)
        qv_in = f_pool[:, 4096:6144].rearrange("p (s w d) -> p s w d", s=2, w=2)

        started = sem("started")

        def apart(eng):
            eng.nop(nofuse=True)

        EARLY = 4
        XG = 7
        spare = acc[:, EARLY * XG:TILES, :].rearrange("p t d -> p (t d)")
        e_rows = spare[:, 0:3 * CHUNKS].bitcast(I32).rearrange("p (a b e) -> p a b e", a=3, b=ROWBLOCKS)
        e_rowsf = spare[:, 2688:2688 + 2 * CHUNKS].rearrange("p (a b e) -> p a b e", a=2, b=ROWBLOCKS)
        unsorted_at = spare[:, 4480:4480 + CHUNKS].rearrange("p (b e) -> p b e", b=ROWBLOCKS)
        HT = TILES + 1
        hot = spare[:, 5376:5376 + HB * (P + HT)].bitcast(BF16)
        hot_lo = hot[:, 0:2 * HB * P].rearrange("p (s c n) -> p s c n", s=2, c=HB)
        hot_hi = hot[:, 2 * HB * P:2 * HB * (P + HT)].rearrange("p (s c n) -> p s c n", s=2, c=HB)
        wv_in = spare[:, 8192:10240].rearrange("p (c d) -> p c d", c=KD)
        wq_in = f_pool[:, 3584:5632].rearrange("p (c d) -> p c d", c=KD)
        b_in = f_pool[:, 5632:6656].rearrange("p (w d) -> p w d", w=2)
        i_lo = f_pool[:, 0:CHUNKS].bitcast(I32)
        i_hi = f_pool[:, 896:896 + CHUNKS].bitcast(I32)
        i_all = spare[:, 2688:2688 + CHUNKS].bitcast(I32)
        f_lo = f_pool[:, 1792:1792 + CHUNKS]
        f_hi = f_pool[:, 2688:2688 + CHUNKS]
        iota_bf = f_pool[:, 6656:6720].bitcast(BF16)
        ones = f_pool[:, 6720:6848]
        cnt = f_pool[:, 0:TILES]
        cums = f_pool[:, 64:64 + TILES]
        cum_i = f_pool[:, 128:128 + TILES].bitcast(I32)
        met_i = f_pool[:, 192:192 + TILES].bitcast(I32)
        rank = f_pool[:, 256:256 + TILES]
        cmp_t = f_pool[:, 320:320 + TCOLS * (TILES - 1)].rearrange("p (c t) -> p c t", c=TCOLS)
        step_no = f_pool[:, 6848:6848 + TCOLS]
        half = f_pool[:, 6856:6856 + TILES]
        zeros = f_pool[:, 6912:6912 + TILES]
        t_f = f_pool[:, 6976:6976 + TCOLS]
        g_f = f_pool[:, 6984:6984 + TCOLS]
        off_f = f_pool[:, 6992:6992 + TCOLS]
        tab_i = f_pool[:, 7000:7000 + 2 * TCOLS].bitcast(I32).rearrange("p (w c) -> p w c", w=2)
        unsorted = small[:, 0:1]
        deg = f_pool[:, 7104:7104 + TILES]

        ld_rows, ld_w, ld_b = sem("ld_rows"), sem("ld_w"), sem("ld_b")
        ld_xe, ld_xl = sem("ld_xe"), sem("ld_xl")
        consts, consts_v = sem("consts"), sem("consts_v")
        chain0 = sem("chain0")
        rows_f, rows_t = sem("rows_f"), sem("rows_t")
        lo_built, hi_built, counted = sem("lo_built"), sem("hi_built"), sem("counted")
        cnt_ready, summed = sem("cnt_ready"), sem("summed")
        unsorted_rows, unsorted_all = sem("unsorted_rows"), sem("unsorted_all")
        deg_ready, dinv_ready, table_ready = sem("deg_ready"), sem("dinv_ready"), sem("table_ready")
        tab_stored, tab_loaded = sem("tab_stored"), sem("tab_loaded")
        y_act, y_dve, y_stored = sem("y_act"), sem("y_dve"), sem("y_stored")
        w_hi, w_lo, b_hi = sem("w_hi"), sem("w_lo"), sem("b_hi")

        with nc.Block() as block:
            @block.sync
            def _(sp):
                sp.sem_inc(started, 1)
                chunk_rows = lambda a, o: a[o:o + EPAD].rearrange("(b p e) -> p b e", p=P, e=P)
                sp.dma_start(e_rows[:, 0], chunk_rows(src, 0)).then_inc(ld_rows, 16)
                sp.dma_start(e_rows[:, 1], chunk_rows(dst, 0)).then_inc(ld_rows, 16)
                sp.dma_start(e_rows[:, 2], chunk_rows(dst, 1)).then_inc(ld_rows, 16)
                sp.dma_start(wq_in, Wq.rearrange("(c p) d -> p c d", p=P)).then_inc(ld_w, 16)
                sp.dma_start(wv_in, Wv.rearrange("(c p) d -> p c d", p=P)).then_inc(ld_w, 16)
                for q in (0, 32):
                    for w, b in enumerate((bq, bv)):
                        sp.dma_start(b_in[q:q + 1, w, :], b[None, :]).then_inc(ld_b, 16)
                for g in range(EARLY):
                    sp.dma_start(acc[:, XG * g:XG * g + XG, :], x_r[:, XG * g:XG * g + XG, :]).then_inc(ld_xe, 16)
                sp.wait_ge(cnt_ready, 1)
                sp.wait_ge(w_lo, 2)
                sp.wait_ge(unsorted_rows, 1)
                for g in range(EARLY, TILES // XG):
                    sp.dma_start(acc[:, XG * g:XG * g + XG, :], x_r[:, XG * g:XG * g + XG, :]).then_inc(ld_xl, 16)
                sp.wait_ge(table_ready, 3)
                for w in range(2):
                    sp.dma_start(tab_dram[w].rearrange("(p c) -> p c", p=P), tab_i[:, w, :]).then_inc(tab_stored, 16)
                sp.dma_start(off_dram[0].rearrange("(p c) -> p c", p=P), off_f).then_inc(tab_stored, 16)
                sp.wait_ge(tab_stored, 48)
                sp.dma_start(tab, tab_dram[None, :, 0:STEPS]).then_inc(tab_loaded, 16)
                sp.dma_start(off_t, off_dram[0:1, 0:STEPS].to_broadcast([P, STEPS])).then_inc(tab_loaded, 16)
                for g in range(TILES // XG):
                    sp.wait_ge(y_act, 3 * (g + 1))
                    sp.wait_ge(y_dve, 4 * (g + 1))
                    sp.dma_start(y_r[:, XG * g:XG * g + XG, :], acc[:, XG * g:XG * g + XG, :]).then_inc(y_stored, 16)
                sp.wait_ge(tab_loaded, 32)
                sp.wait_ge(y_stored, 16 * (TILES // XG))

            @block.gpsimd
            def _(pool):
                pool.iota(iota_row[:], [[1, P]], base=0, channel_multiplier=0,
                          allow_small_or_imprecise_dtypes=True).then_inc(consts, 1)
                pool.iota(iota_bf, [[1, P]], base=0, channel_multiplier=0,
                          allow_small_or_imprecise_dtypes=True).then_inc(consts, 1)
                pool.iota(step_no, [[1, TCOLS]], base=0, channel_multiplier=TCOLS,
                          allow_small_or_imprecise_dtypes=True).then_inc(consts, 1)
                pool.memset(ident[:], 0.0).then_inc(consts, 1)
                pool.wait_ge(consts, 4)
                pool.affine_select(out=ident[:], in_=ident[:], compare_op=ALU.not_equal, fill=1.0, base=0,
                                   pattern=[[-1, P]], channel_multiplier=1).then_inc(consts, 1)
                pool.memset(half, -0.5).then_inc(consts, 1)
                pool.wait_ge(consts, 6)
                pool.wait_ge(deg_ready, 1)
                pool.tensor_tensor(dinv[:], deg, half, ALU.pow).then_inc(dinv_ready, 1)
                pool.wait_ge(unsorted_rows, 1)
                pool.partition_all_reduce(small[:, 1:2], unsorted, P, bass.bass_isa.ReduceOp.max).then_inc(unsorted_all, 1)

            @block.scalar
            def _(act):
                for w, w_in in enumerate((wq_in, wv_in)):
                    act.wait_ge(ld_w, 32)
                    act.activation(w_split[:, w, 0], w_in, ACT.Copy).then_inc(w_hi, 1)
                act.wait_ge(consts_v, 2)
                act.wait_ge(ld_b, 64)
                act.activation(biases[0:1], b_in[0:1], ACT.Copy).then_inc(b_hi, 1)
                act.activation(biases[32:33], b_in[32:33], ACT.Copy).then_inc(b_hi, 1)
                act.wait_ge(dinv_ready, 1)
                for t in range(TILES):
                    if t % XG < 3:
                        g = t // XG
                        if t % XG == 0:
                            act.wait_ge(ld_xe if g < EARLY else ld_xl, 16 * (EARLY if g < EARLY else TILES // XG - EARLY))
                        act.activation(acc[:, t, :], acc[:, t, :], ACT.Copy, scale=dinv[:, t:t + 1]).then_inc(y_act, 1)

            @block.tensor
            def _(pe):
                pe.wait_ge(consts, 5)
                pe.wait_ge(rows_f, 1)
                for a in range(2):
                    for b in range(ROWBLOCKS):
                        last = pe.transpose(bank[2 * a + b // 4][:, (b % 4) * P:(b % 4) * P + P], e_rowsf[:, a, b, :], ident[:])
                last.then_inc(rows_t, 1)
                def count(b, par, start, stop):
                    for c in range(HB):
                        last = pe.matmul(bank[4][:, 0:TILES], hot_lo[:, par, c, :], hot_hi[:, par, c, 0:TILES],
                                         start=start and c == 0, stop=stop and c == HB - 1, skip_group_check=True)
                    last.then_inc(counted, 1)
                pe.wait_ge(lo_built, HB)
                pe.wait_ge(hi_built, 1)
                count(0, 0, True, False)
                with pe.Fori(0, HBATCHES // 2 - 1) as r:
                    for u in range(2):
                        pe.wait_ge(lo_built, r * (2 * HB) + HB * (u + 2))
                        pe.wait_ge(hi_built, r * 2 + u + 2)
                        count(None, 1 - u, False, False)
                pe.wait_ge(lo_built, HB * HBATCHES)
                pe.wait_ge(hi_built, HBATCHES)
                count(HBATCHES - 1, 1, False, True)
                pe.wait_ge(cnt_ready, 1)
                pe.matmul(bank[5][:, 0:TILES], ones, cnt, start=True, stop=True).then_inc(summed, 1)

            @block.vector
            def _(dve):
                done = [0]

                def link(i):
                    done[0] += 1
                    i.then_inc(chain0, 1)
                    dve.wait_ge(chain0, done[0])

                link(dve.memset(ones, 1.0))
                link(dve.memset(zeros, 0.0))
                link(dve.memset(biases.bitcast(F32), 0.0))
                dve.memset(ones_row.bitcast(F32), 0.0).then_inc(consts_v, 1)
                dve.wait_ge(consts_v, 1)
                dve.tensor_copy(ones_row[0:1], ones[0:1]).then_inc(consts_v, 1)
                link(dve.tensor_copy(ones_row[32:33], ones[32:33]))
                dve.wait_ge(ld_rows, 48)
                dve.tensor_copy(e_rowsf, e_rows[:, 0:2]).then_inc(rows_f, 1)
                link(dve.tensor_tensor(unsorted_at, e_rows[:, 1], e_rows[:, 2], ALU.is_gt))
                dve.tensor_reduce(unsorted, unsorted_at, AX.XY, ALU.max).then_inc(unsorted_rows, 1)
                dve.wait_ge(rows_t, 1)
                for a, to in ((0, edges[:, :, 0]), (1, i_all), (1, edges[:, :, 1].bitcast(F32))):
                    dve.tensor_copy(to[:, 0:4 * P], bank[2 * a][:]).then_inc(chain0, 1)
                    dve.tensor_copy(to[:, 4 * P:CHUNKS], bank[2 * a + 1][:, 0:CHUNKS - 4 * P]).then_inc(chain0, 1)
                    done[0] += 2
                dve.wait_ge(chain0, done[0])
                link(dve.tensor_scalar(i_lo, i_all, P - 1, None, ALU.bitwise_and))
                link(dve.tensor_scalar(i_hi, i_all, int(math.log2(P)), None, ALU.logical_shift_right))
                link(dve.tensor_copy(f_lo, i_lo))
                link(dve.tensor_copy(f_hi, i_hi))
                dve.wait_ge(consts, 2)
                def hot_batch(b, par):
                    dve.tensor_tensor(hot_hi[:, par, :, 0:TILES],
                                      f_hi[:, bass.ds(b * HB, HB)].unsqueeze(2).to_broadcast([P, HB, TILES]),
                                      iota_row[:, 0:TILES].unsqueeze(1).to_broadcast([P, HB, TILES]),
                                      ALU.is_equal).then_inc(hi_built, 1)
                    for c in range(HB):
                        dve.tensor_scalar(hot_lo[:, par, c, :], iota_bf, f_lo[:, bass.ds(b * HB + c, 1)], None,
                                          ALU.is_equal).then_inc(lo_built, 1)
                hot_batch(0, 0)
                hot_batch(1, 1)
                with dve.Fori(0, HBATCHES // 2 - 1) as r:
                    for par in range(2):
                        dve.wait_ge(counted, r * 2 + par + 1)
                        hot_batch(r * 2 + par + 2, par)
                dve.wait_ge(counted, HBATCHES)
                dve.tensor_copy(cnt, bank[4][:, 0:TILES]).then_inc(cnt_ready, 1)
                dve.wait_ge(cnt_ready, 1)
                dve.wait_ge(consts, 6)
                link(dve.tensor_scalar(deg, cnt, 1.0, 1e-12, ALU.add, ALU.max))
                dve.sem_inc(deg_ready, 1)
                for w, w_in in enumerate((wq_in, wv_in)):
                    dve.wait_ge(w_hi, w + 1)
                    dve.tensor_tensor(w_split[:, w, 1], w_in, w_split[:, w, 0].bitcast(F32), ALU.subtract).then_inc(w_lo, 1)
                dve.wait_ge(b_hi, 2)
                link(dve.tensor_tensor(biases[32:33], b_in[32:33], biases[32:33].bitcast(F32), ALU.subtract))
                dve.wait_ge(summed, 1)
                link(dve.tensor_tensor_scan(cums, bank[5][:, 0:TILES], zeros, 0.0, ALU.add, ALU.add))
                link(dve.tensor_copy(cum_i, cums))
                link(dve.tensor_scalar(met_i, cum_i, int(math.log2(L)), None, ALU.logical_shift_right))
                link(dve.tensor_copy(rank, met_i))
                link(dve.tensor_tensor(rank[:, 0:TILES - 1], rank[:, 0:TILES - 1], iota_row[:, 1:TILES], ALU.add))
                link(dve.tensor_tensor(cmp_t, rank[:, 0:TILES - 1].unsqueeze(1).to_broadcast([P, TCOLS, TILES - 1]),
                                       step_no.unsqueeze(2).to_broadcast([P, TCOLS, TILES - 1]), ALU.is_le))
                link(dve.tensor_reduce(t_f, cmp_t, AX.X, ALU.add))
                link(dve.tensor_tensor(g_f, step_no, t_f, ALU.subtract))
                dve.tensor_copy(tab_i[:, 0, :], t_f).then_inc(table_ready, 1)
                dve.tensor_copy(tab_i[:, 1, :], g_f).then_inc(table_ready, 1)
                dve.wait_ge(unsorted_all, 1)
                link(dve.tensor_scalar(small[:, 2:3], small[:, 1:2], FAR, None, ALU.mult))
                dve.tensor_scalar(off_f, t_f, float(P), small[:, 2:3], ALU.mult, ALU.add).then_inc(table_ready, 1)
                dve.wait_ge(dinv_ready, 1)
                for t in range(TILES):
                    if t % XG >= 3:
                        g = t // XG
                        if t % XG == 3:
                            dve.wait_ge(ld_xe if g < EARLY else ld_xl, 16 * (EARLY if g < EARLY else TILES // XG - EARLY))
                        dve.tensor_scalar(acc[:, t, :], acc[:, t, :], dinv[:, t:t + 1], None, ALU.mult).then_inc(y_dve, 1)

        col_ready, gathered = sem("col_ready"), [sem(f"gathered{r}") for r in range(RING)]
        g_hi, g_lo, summed_up, added = sem("g_hi"), sem("g_lo"), sem("summed_up"), sem("added")

        class Steps:

            def __init__(self, phase):
                self.n = PHASE_STEPS[phase]
                self.units = self.n * UNITS
                self.base = TILES * sum(PHASE_STEPS[:phase])
                assert 2 * self.units % RING == 0 and self.n * 2 % 2 == 0
                before = [sum(len(range(r, TILES * n * UNITS, RING)) for n in PHASE_STEPS[:phase]) for r in range(RING)]
                self.uses = before

            def step(self, off, pair, k):
                return self.base + off * self.n + k + pair * (2 * self.n)

            def unit(self, off, pair, j):
                c = off * self.units + j
                return self.base * UNITS + c + pair * (2 * self.units), c

            def values(self, engine, row, first, count, top):
                _, v = nc.values_load_multi_w_load_instructions(
                    tab[0:1, row, bass.ds(first, count)], [engine], min_val=0, max_val=top)
                return v

            def pool_turn(self, pool, off, pair):
                groups = self.values(ENG.Pool, 1, self.step(off, pair, 0), self.n, CHUNKS // (K * UNITS) - 1)
                for j in range(self.units):
                    u, c = self.unit(off, pair, j)
                    slot = c % RING
                    if not (isinstance(pair, int) and c < RING):
                        pool.wait_ge(g_lo, (u - RING + 1) * (K + 1))
                        apart(pool)
                    pool.tensor_copy(stage[:, slot], edges[:, bass.ds(groups[j // UNITS] * (K * UNITS) + j % UNITS * K, K), :]
                                     ).then_inc(col_ready, 1)
                    pool.wait_ge(col_ready, u + 1)
                    apart(pool)
                    for k in range(K):
                        pool.indirect_dma_start(gath[:, slot, k * D:k * D + D], None, y_dram,
                                                bass.IndirectOffsetOnAxis(ap=stage[:, slot, k, 0:1], axis=0)
                                                ).then_inc(gathered[slot], 16)

            def act_unit(self, act, off, pair, j):
                u, c = self.unit(off, pair, j)
                slot = c % RING
                act.wait_ge(gathered[slot], (self.uses[slot] + c // RING + 1 + pair * (2 * self.units // RING)) * (16 * K))
                if not (isinstance(pair, int) and c < 2):
                    act.wait_ge(summed_up, u - 1)
                act.activation(g_hl[:, c % 2, 0], gath[:, slot], ACT.Copy).then_inc(g_hi, 1)

            def dve_unit(self, dve, off, pair, j, tiles):
                u, c = self.unit(off, pair, j)
                slot = c % RING
                s = self.step(off, pair, j // UNITS)
                dve.wait_ge(col_ready, u + 1)
                if not (isinstance(pair, int) and c < 2):
                    dve.wait_ge(summed_up, u - 1)
                for k in range(K):
                    dve.tensor_scalar(onehot[:, c % 2, k, :], iota_row[:], off_t[:, bass.ds(s, 1)],
                                      stage[:, slot, k, 1:2].bitcast(F32), ALU.add, ALU.is_equal).then_inc(g_lo, 1)
                dve.wait_ge(g_hi, u + 1)
                dve.tensor_tensor(g_hl[:, c % 2, 1], gath[:, slot], g_hl[:, c % 2, 0].bitcast(F32),
                                  ALU.subtract).then_inc(g_lo, 1)
                if j % UNITS == 0 and c > 0:
                    self.add(dve, s - 1, (c // UNITS - 1) % 2, tiles[j // UNITS])

            def add(self, dve, s, half, t):
                dve.wait_ge(summed_up, (s + 1) * UNITS)
                if not (isinstance(s, int) and s == 0):
                    dve.wait_ge(added, s)
                dve.tensor_tensor(row_tile(acc, t), row_tile(acc, t), agg_bank[half][:], ALU.add).then_inc(added, 1)

            def dve_tiles(self, off, pair):
                if isinstance(pair, int) and off == 0:
                    return (None,) + (tuple(self.values(ENG.DVE, 0, self.base, self.n - 1, TILES - 1)) if self.n > 1 else ())
                return self.values(ENG.DVE, 0, self.step(off, pair, 0) - 1, self.n, TILES - 1)

            def dve_last(self, dve):
                s = self.base + TILES * self.n - 1
                self.add(dve, s, (TILES * self.n - 1) % 2, self.values(ENG.DVE, 0, s, 1, TILES - 1)[0])

            def pe_unit(self, pe, off, pair, j):
                u, c = self.unit(off, pair, j)
                pe.wait_ge(g_lo, (u + 1) * (K + 1))
                if j % UNITS == 0 and not (isinstance(pair, int) and c < 2 * UNITS):
                    pe.wait_ge(added, self.step(off, pair, j // UNITS) - 1)
                for k in range(K):
                    for h in range(2):
                        last = pe.matmul(agg_bank[c // UNITS % 2][:], onehot[:, c % 2, k, :], g_hl[:, c % 2, h, k * D:k * D + D],
                                         start=j % UNITS == 0 and k == 0 and h == 0,
                                         stop=j % UNITS == UNITS - 1 and k == K - 1 and h == 1)
                last.then_inc(summed_up, 1)

        def row_tile(a, i):
            return a[:, bass.ds(i, 1), :].rearrange("p a d -> p (a d)")

        def for_turns2(eng, turn, lag):
            for i in range(3):
                turn(i, 0)
            with eng.Fori(1, (TILES - 1) // 2) as r:
                turn(1, r)
                turn(2, r)
            for i in range(TILES, TILES + lag):
                turn(i, 0)

        def has2(off, pair, lag):
            return not isinstance(pair, int) or 0 <= off - lag < TILES

        def wait(eng, semaphore, value):
            if not (isinstance(value, int) and value <= 0):
                eng.wait_ge(semaphore, value)

        x_loaded = [sem(f"x_loaded{b}") for b in range(2)]
        x_turned, x_hi, x_lo = sem("x_turned"), sem("x_hi"), sem("x_lo")
        q_mul, v_mul, q_relu, q_stat, q_done, v_done = (
            sem("q_mul"), sem("v_mul"), sem("q_relu"), sem("q_stat"), sem("q_done"), sem("v_done"))
        q_stored = [sem(f"q_stored{b}") for b in range(2)]
        v_stored = [sem(f"v_stored{b}") for b in range(2)]
        steps1 = Steps(0)
        bn6 = small[:, 8:14]
        mean_var = small[:, 14:16]
        neg_mean = small[:, 16:18]

        with nc.Block() as block:
            @block.sync
            def _(sp):
                def turn(off, pair):
                    i, par = off + pair * 2, off % 2
                    if has2(off, pair, 0):
                        wait(sp, x_turned, i - 1)
                        sp.dma_start(x_in[:, par], row_tile(x_r, i)).then_inc(x_loaded[par], 16)
                    if has2(off, pair, 2):
                        sp.wait_ge(v_done, i - 1)
                        sp.dma_start(row_tile(v_r, i - 2), v_out[:, par]).then_inc(v_stored[par], 16)
                    if has2(off, pair, 3):
                        sp.wait_ge(q_done, i - 2)
                        sp.dma_start(row_tile(q_r, i - 3), q_out[:, 1 - par]).then_inc(q_stored[1 - par], 16)
                for_turns2(sp, turn, 3)
                for b in range(2):
                    sp.wait_ge(q_stored[b], 16 * ((TILES + 1 - b) // 2))
                    sp.wait_ge(v_stored[b], 16 * ((TILES + 1 - b) // 2))

            @block.gpsimd
            def _(pool):
                for_turns2(pool, lambda off, pair: steps1.pool_turn(pool, off, pair), 0)

            @block.scalar
            def _(act):
                def turn(off, pair):
                    i, par = off + pair * 2, off % 2
                    for j in range(steps1.units):
                        if has2(off, pair, 0):
                            steps1.act_unit(act, off, pair, j)
                        if j == 2 and has2(off, pair, 2):
                            act.wait_ge(q_stat, (i - 2) * 4 + 3)
                            act.activation(q_out[:, par], q_out[:, par], ACT.Relu, bias=neg_mean[:, par:par + 1],
                                           accum_out=s0[:, bass.ds(i - 2, 1)]).then_inc(q_done, 1)
                        if j == 3 and has2(off, pair, 0):
                            act.wait_ge(x_turned, i + 1)
                            wait(act, v_mul, i - 1)
                            act.activation(x_hl[:, par, 0], bank[0][:], ACT.Copy).then_inc(x_hi, 1)
                        if j == 3 and has2(off, pair, 1):
                            act.wait_ge(q_mul, i)
                            b = 1 - par
                            wait(act, q_stored[b], (pair + (off - 1) // 2) * 16)
                            act.activation(q_out[:, b], bank[1][:], ACT.Relu).then_inc(q_relu, 1)
                    if has2(off, pair, 1):
                        b = 1 - par
                        act.wait_ge(v_mul, i)
                        wait(act, v_stored[b], (pair + (off - 1) // 2) * 16)
                        act.activation(v_out[:, b], bank[2][:], ACT.Copy).then_inc(v_done, 1)
                for_turns2(act, turn, 2)

            @block.tensor
            def _(pe):
                def project(w, part, par):
                    dest = bank[1 + w]
                    if part == 0:
                        pe.matmul(dest[:], ones_row, biases[:, w, :], start=True, stop=False)
                    for c in range(KD // 2 * part, KD // 2 * (part + 1)):
                        for a, b in ((0, 0), (0, 1), (1, 0)):
                            last = pe.matmul(dest[:], x_hl[:, par, a, c * P:c * P + P], w_split[:, w, b, c, :],
                                             start=False, stop=c == KD - 1 and a == 1)
                    if part == 1:
                        last.then_inc((q_mul, v_mul)[w], 1)

                def turn(off, pair):
                    i, par = off + pair * 2, off % 2
                    for j in range(steps1.units):
                        if has2(off, pair, 0):
                            steps1.pe_unit(pe, off, pair, j)
                        if j < 4 and has2(off, pair, 1):
                            if j == 0:
                                pe.wait_ge(x_lo, i)
                                wait(pe, q_relu, i - 1)
                            if j == 2:
                                wait(pe, v_done, i - 1)
                            project(j // 2, j % 2, 1 - par)
                        if j == 1 and has2(off, pair, 0):
                            pe.wait_ge(x_loaded[par], (off // 2 + pair + 1) * 16)
                            wait(pe, x_lo, i)
                            for c in range(KD):
                                last = pe.transpose(bank[0][:, c * P:c * P + P], x_in[:, par, c * P:c * P + P], ident[:])
                            last.then_inc(x_turned, 1)
                for_turns2(pe, turn, 1)

            @block.vector
            def _(dve):
                def turn(off, pair):
                    i, par = off + pair * 2, off % 2
                    if has2(off, pair, 0):
                        tiles = steps1.dve_tiles(off, pair)
                    for j in range(steps1.units):
                        if has2(off, pair, 0):
                            steps1.dve_unit(dve, off, pair, j, tiles)
                        if j == 1 and has2(off, pair, 2):
                            m = i - 2
                            dve.wait_ge(q_relu, m + 1)
                            dve.bn_stats(bn6, q_out[:, par]).then_inc(q_stat, 1)
                            dve.wait_ge(q_stat, m * 4 + 1)
                            apart(dve)
                            dve.bn_aggr(mean_var, bn6).then_inc(q_stat, 1)
                            dve.wait_ge(q_stat, m * 4 + 2)
                            wait(dve, q_done, m - 1)
                            dve.tensor_scalar(neg_mean[:, par:par + 1], mean_var[:, 0:1], -1.0, None, ALU.mult).then_inc(q_stat, 1)
                            dve.tensor_copy(var_q[:, bass.ds(m, 1)], mean_var[:, 1:2]).then_inc(q_stat, 1)
                        if j == 3 and has2(off, pair, 0):
                            dve.wait_ge(x_hi, i + 1)
                            wait(dve, v_mul, i - 1)
                            dve.tensor_tensor(x_hl[:, par, 1], bank[0][:], x_hl[:, par, 0].bitcast(F32), ALU.subtract).then_inc(x_lo, 1)
                for_turns2(dve, turn, 2)
                steps1.dve_last(dve)

        chain1, rstd_ready, extremes, angles, valid_ready = (
            sem("chain1"), sem("rstd_ready"), sem("extremes"), sem("angles"), sem("valid_ready"))
        sines = sem("sines")
        scr = f_pool[:, 4096:4096 + 16 * 64].rearrange("p (n t) -> p n t", t=64)
        var_eps, halves, node_no, valid, rs, h2, hang, turns, r1, r2, r3, sin_in, trig, hmm = (
            scr[:, n, 0:TILES] for n in range(14))
        ext = small[:, 20:22]
        ext_all = small[:, 22:24]
        mfac = small[:, 24:28]
        TWO_PI = 2 * math.pi
        PI_A = 6.28125
        PI_B = float(int((TWO_PI - PI_A) * 2**21) / 2**21)
        PI_C = TWO_PI - PI_A - PI_B
        ROUND = 1.5 * 2**23

        with nc.Block() as block:
            @block.gpsimd
            def _(pool):
                pool.iota(node_no, [[P, TILES]], base=0, channel_multiplier=1,
                          allow_small_or_imprecise_dtypes=True).then_inc(valid_ready, 1)
                pool.memset(halves, -0.5).then_inc(valid_ready, 1)
                pool.wait_ge(valid_ready, 2)
                pool.wait_ge(rstd_ready, 1)
                pool.tensor_tensor(rstd[:], var_eps, halves, ALU.pow).then_inc(rstd_ready, 1)
                pool.wait_ge(extremes, 1)
                pool.partition_all_reduce(ext_all, ext, P, bass.bass_isa.ReduceOp.max).then_inc(extremes, 1)

            @block.vector
            def _(dve):
                done = [0]

                def link(i):
                    done[0] += 1
                    i.then_inc(chain1, 1)
                    dve.wait_ge(chain1, done[0])

                dve.tensor_scalar(var_eps, var_q[:, 0:TILES], EPS_LN, None, ALU.add).then_inc(rstd_ready, 1)
                dve.wait_ge(valid_ready, 1)
                link(dve.tensor_scalar(valid, node_no, float(N), None, ALU.is_lt))
                dve.wait_ge(rstd_ready, 2)
                link(dve.tensor_tensor(rs, rstd[:], s0[:], ALU.mult))
                link(dve.tensor_tensor(h2, rs, rs, ALU.mult))
                link(dve.tensor_tensor(hmm, h2, valid, ALU.mult))
                link(dve.tensor_reduce(ext[:, 0:1], hmm, AX.X, ALU.max))
                link(dve.tensor_scalar(r1, valid, 1.0, -3e38, ALU.subtract, ALU.mult))
                link(dve.tensor_tensor(r2, hmm, r1, ALU.add))
                link(dve.tensor_reduce(r3[:, 0:1], r2, AX.X, ALU.min))
                dve.tensor_scalar(ext[:, 1:2], r3[:, 0:1], -1.0, None, ALU.mult).then_inc(extremes, 1)
                dve.wait_ge(extremes, 2)
                link(dve.tensor_tensor(mfac[:, 0:1], ext_all[:, 0:1], ext_all[:, 1:2], ALU.add))
                link(dve.tensor_scalar(mfac[:, 1:2], mfac[:, 0:1], 4.0, None, ALU.mult))
                link(dve.reciprocal(mfac[:, 2:3], mfac[:, 1:2]))
                link(dve.tensor_scalar(mfac[:, 3:4], mfac[:, 2:3], math.pi, None, ALU.mult))
                link(dve.tensor_scalar(hang, h2, mfac[:, 3:4], None, ALU.mult))
                for f, shift in enumerate((0.25, 0.0)):
                    link(dve.tensor_scalar(turns, hang, 1 / TWO_PI, shift, ALU.mult, ALU.add))
                    link(dve.tensor_scalar(r1, turns, ROUND, None, ALU.add))
                    link(dve.tensor_scalar(turns, r1, -ROUND, None, ALU.add))
                    link(dve.scalar_tensor_tensor(r1, turns, -PI_A, hang, ALU.mult, ALU.add))
                    link(dve.scalar_tensor_tensor(r2, turns, -PI_B, r1, ALU.mult, ALU.add))
                    link(dve.scalar_tensor_tensor(r3, turns, -PI_C, r2, ALU.mult, ALU.add))
                    link(dve.tensor_scalar(r1, r3, shift * TWO_PI, math.pi, ALU.add, ALU.min))
                    dve.tensor_scalar(sin_in, r1, -math.pi, None, ALU.max).then_inc(angles, 1)
                    dve.wait_ge(sines, f + 1)
                    link(dve.tensor_tensor(r1, trig, rstd[:], ALU.mult))
                    link(dve.tensor_tensor(r2, r1, valid, ALU.mult))
                    link(dve.tensor_copy(cs[:, :, 2 * f], r2))
                    link(dve.tensor_copy(cs[:, :, 2 * f + 1], r2))
                    link(dve.tensor_copy(cs_split[:, :, f, 0], r2))
                    link(dve.tensor_tensor(cs_split[:, :, f, 1], r2, cs_split[:, :, f, 0].bitcast(F32), ALU.subtract))

            @block.scalar
            def _(act):
                for f in range(2):
                    act.wait_ge(angles, f + 1)
                    act.activation(trig, sin_in, ACT.Sin).then_inc(sines, 1)

        for f in range(2):
            qv_loaded = [sem(f"qv_loaded{f}{b}") for b in range(2)]
            q_hi, v_hi, qv_lo, kv_mul = sem(f"q_hi{f}"), sem(f"v_hi{f}"), sem(f"qv_lo{f}"), sem(f"kv_mul{f}")
            kv_hi, kv_lo = sem(f"kv_hi{f}"), sem(f"kv_lo{f}")
            steps2 = Steps(1 + f)

            with nc.Block() as block:
                @block.sync
                def _(sp, qv_loaded=qv_loaded, qv_lo=qv_lo):
                    def turn(off, pair):
                        i, par = off + pair * 2, off % 2
                        wait(sp, qv_lo, (i - 1) * 2)
                        for w, a in enumerate((q_r, v_r)):
                            sp.dma_start(qv_in[:, par, w], row_tile(a, i)).then_inc(qv_loaded[par], 16)
                    for_turns2(sp, turn, 0)

                @block.gpsimd
                def _(pool, steps2=steps2):
                    for_turns2(pool, lambda off, pair: steps2.pool_turn(pool, off, pair), 0)

                @block.scalar
                def _(act, f=f, steps2=steps2, qv_loaded=qv_loaded, q_hi=q_hi, v_hi=v_hi, kv_mul=kv_mul, kv_hi=kv_hi):
                    def turn(off, pair):
                        i, par = off + pair * 2, off % 2
                        for j in range(steps2.units):
                            steps2.act_unit(act, off, pair, j)
                        act.wait_ge(qv_loaded[par], (off // 2 + pair + 1) * 32)
                        wait(act, kv_mul, i - 1)
                        act.activation(qv_hl[:, par, 0, 0], qv_in[:, par, 0], ACT.Copy).then_inc(q_hi, 1)
                        act.activation(qv_hl[:, par, 1, 0], qv_in[:, par, 1], ACT.Copy,
                                       scale=cs[:, bass.ds(i, 1), 2 * f]).then_inc(v_hi, 1)
                    for_turns2(act, turn, 0)
                    act.wait_ge(kv_mul, TILES)
                    for c in range(KD):
                        act.activation(w_split[:, f, 0, c, :], bank[c][:], ACT.Copy).then_inc(kv_hi, 1)

                @block.tensor
                def _(pe, f=f, steps2=steps2, qv_lo=qv_lo, kv_mul=kv_mul):
                    def turn(off, pair):
                        i, par = off + pair * 2, off % 2
                        if has2(off, pair, 1):
                            first = isinstance(pair, int) and off == 1
                            pe.wait_ge(qv_lo, i * 2)
                        share = KD // steps2.units if steps2.units < KD else 1
                        for j in range(max(steps2.units, KD)):
                            if j < steps2.units and has2(off, pair, 0):
                                steps2.pe_unit(pe, off, pair, j)
                            if not has2(off, pair, 1):
                                continue
                            for c in range(j * share, min(KD, (j + 1) * share)):
                                for a, b in ((0, 0), (0, 1), (1, 0)):
                                    q = qv_hl[:, 1 - par, 0, a, c * P:c * P + P]
                                    pe.matmul(bank[c][:], q, qv_hl[:, 1 - par, 1, b], start=first and a == 0 and b == 0,
                                              stop=True, skip_group_check=True)
                                    if b == 0:
                                        last = pe.matmul(bank[4][:, 2 * c:2 * c + 2], q,
                                                         cs_split[:, bass.ds(i - 1, 1), f, :].rearrange("p a b -> p (a b)"),
                                                         start=first and c == 0 and a == 0, stop=True, skip_group_check=True)
                                if c == KD - 1:
                                    last.then_inc(kv_mul, 1)
                    for_turns2(pe, turn, 1)

                @block.vector
                def _(dve, f=f, steps2=steps2, q_hi=q_hi, v_hi=v_hi, qv_lo=qv_lo, kv_mul=kv_mul, kv_hi=kv_hi, kv_lo=kv_lo):
                    def turn(off, pair):
                        i, par = off + pair * 2, off % 2
                        tiles = steps2.dve_tiles(off, pair)
                        for j in range(steps2.units):
                            steps2.dve_unit(dve, off, pair, j, tiles)
                        dve.wait_ge(q_hi, i + 1)
                        dve.tensor_tensor(qv_hl[:, par, 0, 1], qv_in[:, par, 0], qv_hl[:, par, 0, 0].bitcast(F32),
                                          ALU.subtract).then_inc(qv_lo, 1)
                        dve.wait_ge(v_hi, i + 1)
                        dve.scalar_tensor_tensor(qv_hl[:, par, 1, 1], qv_in[:, par, 1], cs[:, bass.ds(i, 1), 2 * f],
                                                 qv_hl[:, par, 1, 0].bitcast(F32), ALU.mult, ALU.subtract).then_inc(qv_lo, 1)
                    for_turns2(dve, turn, 0)
                    steps2.dve_last(dve)
                    for c in range(KD):
                        dve.wait_ge(kv_hi, c + 1)
                        dve.tensor_tensor(w_split[:, f, 1, c, :], bank[c][:], w_split[:, f, 0, c, :].bitcast(F32),
                                          ALU.subtract).then_inc(kv_lo, 1)
                    qsum = small[:, 32:36]
                    dve.tensor_reduce(qsum, bank[4][:, 0:2 * KD].rearrange("p (c h) -> p c h", h=2), AX.X, ALU.add
                                      ).then_inc(kv_lo, 1)
                    dve.wait_ge(kv_lo, KD + 1)
                    dve.tensor_copy(qn[:, :, 2 * f], qsum).then_inc(kv_lo, 1)
                    dve.wait_ge(kv_lo, KD + 2)
                    dve.tensor_tensor(qn[:, :, 2 * f + 1], qsum, qn[:, :, 2 * f].bitcast(F32), ALU.subtract).then_inc(kv_lo, 1)

        x4 = f_pool[:, 0:2048].rearrange("p (s d) -> p s d", s=4)
        q2 = f_pool[:, 2048:3072].rearrange("p (s d) -> p s d", s=2)
        v2 = f_pool[:, 3072:4096].rearrange("p (s d) -> p s d", s=2)
        u2 = f_pool[:, 4096:5120].rearrange("p (s d) -> p s d", s=2)
        t4 = f_pool[:, 5120:7168].rearrange("p (s d) -> p s d", s=4)
        wg_in = f_pool[:, 0:2048].rearrange("p (c d) -> p c d", c=KD)
        affine = edges[:].rearrange("p c w -> p (c w)")[:, 0:3 * D].bitcast(F32).rearrange("p (a d) -> p a d", a=3)
        z2 = tables[:, 0:2 * D].bitcast(F32).rearrange("p (s d) -> p s d", s=2)
        st1 = small[:, 0:32].rearrange("p (s c) -> p s c", s=2)
        st2 = small[:, 32:64].rearrange("p (s c) -> p s c", s=2)
        nrm = var_q[:, 0:32].rearrange("p (s c) -> p s c", s=2)

        expo = var_q[:, 40:41]

        ld3, wg_hi_done, wg_lo_done, expo_ready = sem("ld3"), sem("wg_hi_done"), sem("wg_lo_done"), sem("expo_ready")
        x3_loaded = [sem(f"x3_loaded{b}") for b in range(4)]
        q3_loaded = [sem(f"q3_loaded{b}") for b in range(2)]
        v3_loaded = [sem(f"v3_loaded{b}") for b in range(2)]
        out_stored = [sem(f"out_stored{b}") for b in range(4)]
        z_made = sem("z_made")
        turned, t_hi, t_lo = sem("turned"), sem("t_hi"), sem("t_lo")
        mul_n, mul_a, mul_b, mul_c = sem("mul_n"), sem("mul_a"), sem("mul_b"), sem("mul_c")
        vb, norms, u_a, u_sum, stat1, stat2 = (
            sem("vb"), sem("norms"), sem("u_a"), sem("u_sum"), sem("stat1"), sem("stat2"))
        rstd1, rstd2, shift1, shift2 = sem("rstd1"), sem("rstd2"), sem("shift1"), sem("shift2")
        normed, scaled, residual, out_done = sem("normed"), sem("scaled"), sem("residual"), sem("out_done")

        def for_turns(eng, body):
            for i in range(6):
                body(i, i // 4, i % 4)
            with eng.Fori(1, (TILES - 2) // 4) as r:
                for n in range(2, 6):
                    body(r * 4 + n, r + n // 4, n % 4)
            for i in range((TILES - 2) // 4 * 4 + 2, TILES + 3):
                body(i, i // 4, i % 4)

        def has(i, lag):
            return not isinstance(i, int) or 0 <= i - lag < TILES

        def after(eng, i, first, semaphore, value):
            if not (isinstance(i, int) and i < first):
                eng.wait_ge(semaphore, value)

        with nc.Block() as block:
            @block.sync
            def _(sp):
                sp.dma_start(wg_in, Wg.rearrange("(c p) d -> p c d", p=P)).then_inc(ld3, 16)
                for n, b in enumerate((gamma, beta, bg)):
                    sp.dma_start(affine[:, n], b[None, :].to_broadcast([P, D])).then_inc(ld3, 16)
                sp.wait_ge(wg_lo_done, 1)

                def turn(i, r, n):
                    if has(i, 0):
                        after(sp, i, 2, turned, i - 1)
                        sp.dma_start(q2[:, n % 2], row_tile(q_r, i)).then_inc(q3_loaded[n % 2], 16)
                        after(sp, i, 4, residual, i - 3)
                        sp.dma_start(x4[:, n], row_tile(x_r, i)).then_inc(x3_loaded[n], 16)
                        after(sp, i, 2, u_sum, (i - 1) * 3)
                        sp.dma_start(v2[:, n % 2], row_tile(v_r, i)).then_inc(v3_loaded[n % 2], 16)
                    if has(i, 4):
                        sp.wait_ge(out_done, i - 3)
                        sp.dma_start(row_tile(out_r, i - 4), t4[:, n]).then_inc(out_stored[n], 16)
                for_turns(sp, turn)
                sp.wait_ge(out_done, TILES)
                sp.dma_start(row_tile(out_r, TILES - 1), t4[:, (TILES - 1) % 4]).then_inc(out_stored[(TILES - 1) % 4], 16)
                for b in range(4):
                    sp.wait_ge(out_stored[b], 16 * len(range(b, TILES, 4)))

            @block.gpsimd
            def _(pool):
                pool.memset(expo, -0.5).then_inc(expo_ready, 1)
                pool.wait_ge(expo_ready, 1)
                pool.wait_ge(ld3, 64)

                def power(i, lag, stat, st, ready):
                    pool.wait_ge(stat, (i - lag + 1) * 2)
                    apart(pool)
                    pool.tensor_scalar(st[:, 8:9], st[:, 7:8], EPS_LN, None, ALU.add).then_inc(ready, 1)
                    pool.wait_ge(ready, (i - lag) * 2 + 1)
                    pool.tensor_tensor(st[:, 8:9], st[:, 8:9], expo, ALU.pow).then_inc(ready, 1)

                def scale_row(i, n):
                    apart(pool)
                    pool.tensor_tensor(z2[:, n % 2], row_tile(acc, i), dinv[:, bass.ds(i, 1)].to_broadcast([P, D]),
                                       ALU.mult).then_inc(z_made, 1)

                scale_row(0, 0)

                def turn(i, r, n):
                    if has(i, -1):
                        after(pool, i, 1, turned, i)
                        scale_row(i + 1, n + 1)
                    if has(i, 0):
                        pool.wait_ge(v3_loaded[n % 2], (r * 2 + n // 2 + 1) * 16)
                        pool.tensor_tensor(v2[:, n % 2], v2[:, n % 2], affine[:, 2], ALU.add).then_inc(vb, 1)
                    if has(i, 3):
                        power(i, 3, stat2, st2[:, (n - 3) % 2], rstd2)
                    if has(i, 2):
                        t = t4[:, (n - 2) % 4]
                        pool.wait_ge(normed, i - 1)
                        pool.tensor_tensor(t, t, affine[:, 0], ALU.mult).then_inc(scaled, 1)
                        pool.wait_ge(scaled, (i - 2) * 2 + 1)
                        pool.tensor_tensor(t, t, affine[:, 1], ALU.add).then_inc(scaled, 1)
                    if has(i, 1):
                        power(i, 1, stat1, st1[:, (n - 1) % 2], rstd1)
                for_turns(pool, turn)

            @block.scalar
            def _(act):
                act.wait_ge(ld3, 64)
                act.activation(wg_hl[:, 0], wg_in, ACT.Copy).then_inc(wg_hi_done, 1)

                def turn(i, r, n):
                    if has(i, 0):
                        act.wait_ge(turned, i + 1)
                        after(act, i, 2, mul_c, i - 1)
                        for w in range(2):
                            act.activation(qz_hl[:, n % 2, w, 0], bank[w][:], ACT.Copy).then_inc(t_hi, 1)
                    if has(i, 2):
                        b = (n - 2) % 4
                        act.wait_ge(shift1, i - 1)
                        after(act, i, 6, out_stored[b], (r + (n - 2) // 4) * 16)
                        s = st1[:, n % 2]
                        act.activation(t4[:, b], u2[:, n % 2], ACT.Identity, bias=s[:, 9:10], scale=s[:, 8:9]).then_inc(normed, 1)
                    if has(i, 1):
                        act.wait_ge(mul_a, i)
                        act.wait_ge(norms, i * 4)
                        after(act, i, 3, normed, i - 2)
                        act.activation(u2[:, (n - 1) % 2], bank[2][:], ACT.Copy, scale=nrm[:, (n - 1) % 2, 6:7]).then_inc(u_a, 1)
                    if has(i, 3):
                        act.wait_ge(shift2, i - 2)
                        s = st2[:, (n - 3) % 2]
                        t = t4[:, (n - 3) % 4]
                        act.activation(t, t, ACT.Identity, bias=s[:, 9:10], scale=s[:, 8:9]).then_inc(out_done, 1)
                for_turns(act, turn)

            @block.tensor
            def _(pe):
                def turn(i, r, n):
                    if has(i, 0):
                        pe.wait_ge(q3_loaded[n % 2], (r * 2 + n // 2 + 1) * 16)
                        after(pe, i, 1, t_lo, i * 2)
                        for c in range(KD):
                            pe.transpose(bank[0][:, c * P:c * P + P], q2[:, n % 2, c * P:c * P + P], ident[:])
                        pe.wait_ge(z_made, i + 1)
                        for c in range(KD):
                            last = pe.transpose(bank[1][:, c * P:c * P + P], z2[:, n % 2, c * P:c * P + P], ident[:])
                        last.then_inc(turned, 1)
                    if has(i, 1):
                        pe.wait_ge(t_lo, i * 2)
                        qz = qz_hl[:, (n - 1) % 2]
                        after(pe, i, 2, norms, i * 4 - 6)
                        for c in range(KD):
                            for h in range(2):
                                last = pe.matmul(bank[5][:, 0:4], qz[:, 0, h, c * P:c * P + P], qn[:, c, :],
                                                 start=c == 0 and h == 0, stop=c == KD - 1 and h == 1)
                        last.then_inc(mul_n, 1)

                        def product(dest, w, weight, mul):
                            for c in range(KD):
                                for a, b in ((0, 0), (0, 1), (1, 0)):
                                    last = pe.matmul(dest[:], qz[:, w, a, c * P:c * P + P], weight(b, c),
                                                     start=c == 0 and a == 0 and b == 0, stop=c == KD - 1 and a == 1)
                            last.then_inc(mul, 1)
                        after(pe, i, 2, u_a, i - 1)
                        product(bank[2], 0, lambda b, c: w_split[:, 0, b, c, :], mul_a)
                        after(pe, i, 2, u_sum, i * 3 - 5)
                        product(bank[3], 0, lambda b, c: w_split[:, 1, b, c, :], mul_b)
                        after(pe, i, 2, u_sum, i * 3 - 4)
                        product(bank[4], 1, lambda b, c: wg_hl[:, b, c, :], mul_c)
                pe.wait_ge(wg_lo_done, 1)
                for_turns(pe, turn)

            @block.vector
            def _(dve):
                dve.wait_ge(wg_hi_done, 1)
                dve.tensor_tensor(wg_hl[:, 1], wg_in, wg_hl[:, 0].bitcast(F32), ALU.subtract).then_inc(wg_lo_done, 1)

                def shift(st, rstd_sem, count, ready):
                    dve.wait_ge(rstd_sem, count)
                    dve.scalar_tensor_tensor(st[:, 9:10], st[:, 6:7], -1.0, st[:, 8:9], ALU.mult, ALU.mult).then_inc(ready, 1)

                def stats(st, a, stat, before):
                    dve.bn_stats(st[:, 0:6], a).then_inc(stat, 1)
                    dve.wait_ge(stat, before + 1)
                    apart(dve)
                    dve.bn_aggr(st[:, 6:8], st[:, 0:6]).then_inc(stat, 1)

                def turn(i, r, n):
                    if has(i, 2):
                        shift(st1[:, n % 2], rstd1, (i - 1) * 2, shift1)
                    if has(i, 0):
                        for w in range(2):
                            dve.wait_ge(t_hi, i * 2 + w + 1)
                            dve.tensor_tensor(qz_hl[:, n % 2, w, 1], bank[w][:], qz_hl[:, n % 2, w, 0].bitcast(F32),
                                              ALU.subtract).then_inc(t_lo, 1)
                    if has(i, 3):
                        b = (n - 3) % 4
                        dve.wait_ge(scaled, (i - 2) * 2)
                        dve.wait_ge(x3_loaded[b], (r + (n - 3) // 4 + 1) * 16)
                        dve.scalar_tensor_tensor(t4[:, b], t4[:, b], 0.0, x4[:, b], ALU.max, ALU.add).then_inc(residual, 1)
                        dve.wait_ge(residual, i - 2)
                        stats(st2[:, (n - 3) % 2], t4[:, b], stat2, (i - 3) * 2)
                    if has(i, 1):
                        s = nrm[:, (n - 1) % 2]
                        u = u2[:, (n - 1) % 2]
                        m = i - 1
                        dve.tensor_copy(s[:, 8:12], cs[:, bass.ds(m, 1), :].rearrange("p a b -> p (a b)")).then_inc(norms, 1)
                        dve.wait_ge(mul_n, i)
                        dve.wait_ge(norms, m * 4 + 1)
                        dve.tensor_tensor_reduce(s[:, 0:4], bank[5][:, 0:4], s[:, 8:12],
                                                 1.0, EPS_NORM, ALU.mult, ALU.add, s[:, 4:5]).then_inc(norms, 1)
                        dve.wait_ge(norms, m * 4 + 2)
                        dve.reciprocal(s[:, 5:6], s[:, 4:5]).then_inc(norms, 1)
                        dve.wait_ge(norms, m * 4 + 3)
                        dve.tensor_scalar(s[:, 6:8], s[:, 8:12:2], s[:, 5:6], None, ALU.mult).then_inc(norms, 1)
                        dve.wait_ge(norms, m * 4 + 4)
                        dve.wait_ge(u_a, i)
                        dve.wait_ge(mul_b, i)
                        dve.scalar_tensor_tensor(u, bank[3][:], s[:, 7:8], u, ALU.mult, ALU.add).then_inc(u_sum, 1)
                        if has(i, 3):
                            shift(st2[:, (n - 3) % 2], rstd2, (i - 2) * 2, shift2)
                        dve.wait_ge(mul_c, i)
                        dve.wait_ge(u_sum, m * 3 + 1)
                        dve.tensor_tensor(u, bank[4][:], u, ALU.add).then_inc(u_sum, 1)
                        dve.wait_ge(vb, i)
                        dve.wait_ge(u_sum, m * 3 + 2)
                        dve.tensor_tensor(u, u, v2[:, (n - 1) % 2], ALU.add).then_inc(u_sum, 1)
                        dve.wait_ge(u_sum, m * 3 + 3)
                        stats(st1[:, (n - 1) % 2], u, stat1, m * 2)
                    elif has(i, 3):
                        shift(st2[:, (n - 3) % 2], rstd2, (i - 2) * 2, shift2)
                for_turns(dve, turn)


def kernel(x, src, dst, L0_gnn_Wq, L0_gnn_bq, L0_gnn_Wv, L0_gnn_bv, L0_gnn_Wg, L0_gnn_bg, L0_gnn_gamma,
           L0_gnn_beta):
    import numpy as np
    import concourse.bacc as bacc
    from concourse.bass_utils import run_bass_kernel_spmd

    xp = np.zeros((NPAD, D), np.float32)
    xp[:N] = np.asarray(x)
    sp = np.zeros(EPAD, np.int32)
    sp[:E] = np.asarray(src)
    dp = np.full(EPAD + P, NPAD, np.int32)
    dp[:E] = np.asarray(dst)
    arrays = {"x": xp, "src": sp, "dst": dp, "Wq": L0_gnn_Wq, "bq": L0_gnn_bq, "Wv": L0_gnn_Wv, "bv": L0_gnn_bv,
              "Wg": L0_gnn_Wg, "bg": L0_gnn_bg, "gamma": L0_gnn_gamma, "beta": L0_gnn_beta}
    arrays = {f"in_{k}": np.ascontiguousarray(a) for k, a in arrays.items()}
    nc = bacc.Bacc("TRN2", target_bir_lowering=False, num_devices=1)
    aps = {k[3:]: nc.dram_tensor(k, a.shape, mybir.dt.from_np(a.dtype), kind="ExternalInput").ap()
           for k, a in arrays.items()}
    out = nc.dram_tensor("out_0", (NPAD, D), F32, kind="ExternalOutput").ap()
    build(nc, out=out, **aps)
    r = run_bass_kernel_spmd(nc, [arrays], core_ids=[0])
    return r.results[0]["out_0"][:N]
```

```python
import math
from contextlib import ExitStack

import concourse.bass as bass
from concourse import mybir

F32 = mybir.dt.float32
F32R = mybir.dt.float32r
BF16 = mybir.dt.bfloat16
I32 = mybir.dt.int32
ALU = mybir.AluOpType
ACT = mybir.ActivationFunctionType
AX = mybir.AxisListType
ENG = mybir.EngineType

P = 128
N = 6250
D = 512
E = 100000
EPS_LN = 1e-5
EPS_NORM = 1e-10
TILES = -(-N // P)
NPAD = TILES * P
KD = D // P
K = 2
UNITS = 1
L = UNITS * K * P
GROUPS = -(-E // L)
PHASE_STEPS = (5, 2, 2)
STEPS = TILES * sum(PHASE_STEPS)
assert STEPS >= GROUPS + TILES - 1
ACT_HOT = (False, True, True)
RINGS = (5, 4, 4)
ROWBLOCKS = -(-(STEPS - TILES + 1) * UNITS * K // P)
CHUNKS = ROWBLOCKS * P
EPAD = CHUNKS * P
HB = 14
ACT_HB = 4
HBATCHES = -(-E // (P * HB))
HLOOP = 6
assert (HBATCHES - 2) % HLOOP == 0 and HBATCHES * HB <= CHUNKS
TCOLS = -(-STEPS // P)
FAR = float(1 << 20)


def build(nc, x, src, dst, Wq, bq, Wv, bv, Wg, bg, gamma, beta, out):
    with ExitStack() as ctx:
        def sb(name, shape, dt):
            return ctx.enter_context(nc.sbuf_tensor("sb_" + name, shape, dt))

        def sem(name):
            return ctx.enter_context(nc.semaphore(name))

        y_dram = nc.dram_tensor("y_scratch", [NPAD, D], F32).ap()
        q_dram = nc.dram_tensor("q_scratch", [NPAD, D], F32).ap()
        v_dram = nc.dram_tensor("v_scratch", [NPAD, D], F32).ap()
        tab_dram = nc.dram_tensor("tab_scratch", [2, TCOLS * P], I32).ap()
        off_dram = nc.dram_tensor("off_scratch", [1, TCOLS * P], F32).ap()

        def rows(a):
            return a.rearrange("(t p) d -> p t d", p=P)

        x_r, y_r, q_r, v_r, out_r = rows(x), rows(y_dram), rows(q_dram), rows(v_dram), rows(out)

        acc = sb("acc", [P, TILES, D], F32)
        edges = sb("edges", [P, CHUNKS, 2], I32)
        w_split = sb("w_split", [P, 2, 2, KD, D], F32R)
        r_pool = sb("r_pool", [P, 8192], F32R)
        f_pool = sb("f_pool", [P, 7168], F32)
        ident = sb("ident", [P, P], F32)
        iota_row = sb("iota_row", [P, P], F32)
        tables = sb("tables", [P, max(3 * STEPS, 2 * D)], I32)
        tab = tables[0:1, 0:2 * STEPS].rearrange("p (w s) -> p w s", w=2)
        off_t = tables[:, 2 * STEPS:3 * STEPS].bitcast(F32)
        stage = sb("stage", [P, max(RINGS), K, 2], I32)
        var_q = sb("var_q", [P, 64], F32)
        s0 = sb("s0", [P, TILES], F32)
        dinv = sb("dinv", [P, TILES], F32)
        rstd = sb("rstd", [P, TILES], F32)
        cs = sb("cs", [P, TILES, 4], F32)
        cs_split = sb("cs_split", [P, TILES, 2, 2], F32R)
        q_col = sb("q_col", [P, 2, KD], F32)
        small = sb("small", [P, 64], F32)
        dst_rel = sb("dst_rel", [P, 2, K], F32)
        bank = [ctx.enter_context(nc.psum_tensor(f"bank{b}", [P, D], F32)) for b in range(8)]
        agg_bank = bank[6:8]

        g_hl = r_pool[:, 0:4096].rearrange("p (s h f) -> p s h f", s=2, h=2)
        x_hl = r_pool[:, 4096:6144].rearrange("p (s h d) -> p s h d", s=2, h=2)
        biases = r_pool[:, 6144:7168].rearrange("p (w d) -> p w d", w=2)
        ones_row = r_pool[:, 7168:7296]
        onehot = r_pool[:, 7296:7296 + 2 * K * P].rearrange("p (s k n) -> p s k n", s=2, k=K)
        qv_hl = w_split[:, 1, :, :, :].rearrange("p h c d -> p (h c d)").rearrange(
            "p (s w h d) -> p s w h d", s=2, w=2, h=2)
        wg_hl = r_pool[:, 0:4096].rearrange("p (h c d) -> p h c d", h=2, c=KD)
        qz_hl = r_pool[:, 4096:8192].rearrange("p (s w h d) -> p s w h d", s=2, w=2, h=2)
        gath = f_pool[:, 0:max(RINGS) * K * D].rearrange("p (s f) -> p s f", s=max(RINGS))
        x_in = f_pool[:, 5120:5632]
        v_out = f_pool[:, 5632:6144]
        q_out = f_pool[:, 6144:7168].rearrange("p (s d) -> p s d", s=2)
        dist = f_pool[:, 6144:6144 + K * P].rearrange("p (k n) -> p k n", k=K)
        qv_in = f_pool[:, 4096:6144].rearrange("p (s w d) -> p s w d", s=2, w=2)

        def apart(eng):
            eng.nop(nofuse=True)

        EARLY = 4
        XG = 7
        spare = acc[:, EARLY * XG:TILES, :].rearrange("p t d -> p (t d)")
        e_rows = spare[:, 0:3 * CHUNKS].bitcast(I32).rearrange("p (a b e) -> p a b e", a=3, b=ROWBLOCKS)
        e_rowsf = spare[:, 2688:2688 + 2 * CHUNKS].rearrange("p (a b e) -> p a b e", a=2, b=ROWBLOCKS)
        unsorted_at = spare[:, 4480:4480 + CHUNKS].rearrange("p (b e) -> p b e", b=ROWBLOCKS)
        HT = TILES + 1
        hot_lo = f_pool[:, 0:HB * P].bitcast(BF16).rearrange("p (s c n) -> p s c n", s=2, c=HB)
        hot_hi = f_pool[:, 3584:3584 + HB * HT].bitcast(BF16).rearrange("p (s c n) -> p s c n", s=2, c=HB)
        hot_dist = f_pool[:, 4352:4352 + ACT_HB * P].bitcast(BF16).rearrange("p (s c n) -> p s c n", s=2, c=ACT_HB)
        wv_in = spare[:, 8192:10240].rearrange("p (c d) -> p c d", c=KD)
        wq_in = f_pool[:, 3584:5632].rearrange("p (c d) -> p c d", c=KD)
        b_in = f_pool[:, 5632:6656].rearrange("p (w d) -> p w d", w=2)
        i_lo = f_pool[:, 0:CHUNKS].bitcast(I32)
        i_hi = f_pool[:, 896:896 + CHUNKS].bitcast(I32)
        i_all = spare[:, 2688:2688 + CHUNKS].bitcast(I32)
        f_lo = f_pool[:, 1792:1792 + CHUNKS]
        f_hi = f_pool[:, 2688:2688 + CHUNKS]
        iota_bf = f_pool[:, 6656:6720].bitcast(BF16)
        ones = f_pool[:, 6720:6848]
        cnt = f_pool[:, 0:TILES]
        cums = f_pool[:, 64:64 + TILES]
        cum_i = f_pool[:, 128:128 + TILES].bitcast(I32)
        met_i = f_pool[:, 192:192 + TILES].bitcast(I32)
        rank = f_pool[:, 256:256 + TILES]
        cmp_t = f_pool[:, 320:320 + TCOLS * (TILES - 1)].rearrange("p (c t) -> p c t", c=TCOLS)
        step_no = f_pool[:, 6848:6848 + TCOLS]
        half = f_pool[:, 6856:6856 + TILES]
        zeros = f_pool[:, 6912:6912 + TILES]
        t_f = f_pool[:, 6976:6976 + TCOLS]
        g_f = f_pool[:, 6984:6984 + TCOLS]
        off_f = f_pool[:, 6992:6992 + TCOLS]
        tab_i = f_pool[:, 7000:7000 + 2 * TCOLS].bitcast(I32).rearrange("p (w c) -> p w c", w=2)
        unsorted = small[:, 0:1]
        deg = f_pool[:, 7104:7104 + TILES]

        ld_rows, ld_w, ld_b = sem("ld_rows"), sem("ld_w"), sem("ld_b")
        ld_xe, ld_xl = sem("ld_xe"), sem("ld_xl")
        consts, consts_v = sem("consts"), sem("consts_v")
        chain0 = sem("chain0")
        rows_f, rows_t = sem("rows_f"), sem("rows_t")
        lo_ready, dist_built, act_built = sem("lo_ready"), sem("dist_built"), sem("act_built")
        lo_built, hi_built, counted = sem("lo_built"), sem("hi_built"), sem("counted")
        cnt_ready, summed = sem("cnt_ready"), sem("summed")
        unsorted_rows, unsorted_all = sem("unsorted_rows"), sem("unsorted_all")
        deg_ready, dinv_ready, table_ready = sem("deg_ready"), sem("dinv_ready"), sem("table_ready")
        tab_stored, tab_loaded = sem("tab_stored"), sem("tab_loaded")
        acc_act, acc_dve, y_stored = sem("acc_act"), sem("acc_dve"), sem("y_stored")
        w_hi, w_lo, b_hi = sem("w_hi"), sem("w_lo"), sem("b_hi")

        def self_act(act, tiles):
            for t in tiles:
                if t % XG < 3:
                    act.activation(acc[:, t, :], acc[:, t, :], ACT.Copy, scale=dinv[:, t:t + 1]).then_inc(acc_act, 1)

        def self_dve(dve, tiles):
            for t in tiles:
                if t % XG >= 3:
                    dve.tensor_scalar(acc[:, t, :], acc[:, t, :], dinv[:, t:t + 1], None, ALU.mult).then_inc(acc_dve, 1)

        with nc.Block() as block:
            @block.sync
            def _(sp):
                chunk_rows = lambda a, o: a[o:o + EPAD].rearrange("(b p e) -> p b e", p=P, e=P)
                sp.dma_start(e_rows[:, 0], chunk_rows(src, 0)).then_inc(ld_rows, 16)
                sp.dma_start(e_rows[:, 1], chunk_rows(dst, 0)).then_inc(ld_rows, 16)
                sp.dma_start(e_rows[:, 2], chunk_rows(dst, 1)).then_inc(ld_rows, 16)
                sp.dma_start(wq_in, Wq.rearrange("(c p) d -> p c d", p=P)).then_inc(ld_w, 16)
                sp.dma_start(wv_in, Wv.rearrange("(c p) d -> p c d", p=P)).then_inc(ld_w, 16)
                for q in (0, 32):
                    for w, b in enumerate((bq, bv)):
                        sp.dma_start(b_in[q:q + 1, w, :], b[None, :]).then_inc(ld_b, 16)
                for g in range(EARLY):
                    sp.dma_start(acc[:, XG * g:XG * g + XG, :], x_r[:, XG * g:XG * g + XG, :]).then_inc(ld_xe, 16)
                sp.wait_ge(w_lo, 2)
                sp.wait_ge(unsorted_rows, 1)
                sp.wait_ge(lo_ready, 1)
                for g in range(EARLY, TILES // XG):
                    sp.dma_start(acc[:, XG * g:XG * g + XG, :], x_r[:, XG * g:XG * g + XG, :]).then_inc(ld_xl, 16)
                sp.wait_ge(table_ready, 3)
                for w in range(2):
                    sp.dma_start(tab_dram[w].rearrange("(p c) -> p c", p=P), tab_i[:, w, :]).then_inc(tab_stored, 16)
                sp.dma_start(off_dram[0].rearrange("(p c) -> p c", p=P), off_f).then_inc(tab_stored, 16)
                sp.wait_ge(tab_stored, 48)
                sp.dma_start(tab, tab_dram[None, :, 0:STEPS]).then_inc(tab_loaded, 16)
                sp.dma_start(off_t, off_dram[0:1, 0:STEPS].to_broadcast([P, STEPS])).then_inc(tab_loaded, 16)
                for g in range(TILES // XG):
                    sp.wait_ge(acc_act, 3 * (g + 1))
                    sp.wait_ge(acc_dve, 4 * (g + 1))
                    sp.dma_start(y_r[:, XG * g:XG * g + XG, :], acc[:, XG * g:XG * g + XG, :]).then_inc(y_stored, 16)
                sp.wait_ge(tab_loaded, 32)

            @block.gpsimd
            def _(pool):
                pool.iota(iota_row[:], [[1, P]], base=0, channel_multiplier=0,
                          allow_small_or_imprecise_dtypes=True).then_inc(consts, 1)
                pool.iota(iota_bf, [[1, P]], base=0, channel_multiplier=0,
                          allow_small_or_imprecise_dtypes=True).then_inc(consts, 1)
                pool.iota(step_no, [[1, TCOLS]], base=0, channel_multiplier=TCOLS,
                          allow_small_or_imprecise_dtypes=True).then_inc(consts, 1)
                pool.memset(ident[:], 0.0).then_inc(consts, 1)
                pool.wait_ge(consts, 4)
                pool.affine_select(out=ident[:], in_=ident[:], compare_op=ALU.not_equal, fill=1.0, base=0,
                                   pattern=[[-1, P]], channel_multiplier=1).then_inc(consts, 1)
                pool.memset(half, -0.5).then_inc(consts, 1)
                pool.wait_ge(consts, 6)
                pool.wait_ge(deg_ready, 1)
                pool.tensor_tensor(dinv[:], deg, half, ALU.pow).then_inc(dinv_ready, 1)
                pool.wait_ge(unsorted_rows, 1)
                pool.partition_all_reduce(small[:, 1:2], unsorted, P, bass.bass_isa.ReduceOp.max).then_inc(unsorted_all, 1)

            @block.scalar
            def _(act):
                for w, w_in in enumerate((wq_in, wv_in)):
                    act.wait_ge(ld_w, 32)
                    act.activation(w_split[:, w, 0], w_in, ACT.Copy).then_inc(w_hi, 1)
                act.wait_ge(consts_v, 2)
                act.wait_ge(ld_b, 64)
                act.activation(biases[0:1], b_in[0:1], ACT.Copy).then_inc(b_hi, 1)
                act.activation(biases[32:33], b_in[32:33], ACT.Copy).then_inc(b_hi, 1)

                act.wait_ge(consts, 2)
                act.wait_ge(lo_ready, 1)
                act.wait_ge(w_lo, 2)
                def hot_batch(b, par):
                    for c in range(ACT_HB):
                        act.activation(hot_dist[:, par, c, :], iota_bf, ACT.Abs, bias=f_lo[:, bass.ds(b * HB + (HB - ACT_HB) + c, 1)],
                                       scale=-1.0).then_inc(dist_built, 1)
                    act.wait_ge(dist_built, b * ACT_HB + ACT_HB)
                    act.activation(hot_lo[:, par, HB - ACT_HB:HB, :], hot_dist[:, par], ACT.Relu, bias=1.0, scale=-1.0
                                   ).then_inc(act_built, 1)
                hot_batch(0, 0)
                hot_batch(1, 1)
                with act.Fori(0, (HBATCHES - 2) // HLOOP) as r:
                    for u in range(HLOOP):
                        act.wait_ge(counted, r * HLOOP + u + 1)
                        act.wait_ge(act_built, r * HLOOP + u + 1)
                        hot_batch(r * HLOOP + u + 2, u % 2)
                act.wait_ge(dinv_ready, 1)
                act.wait_ge(ld_xe, 16 * EARLY)
                act.wait_ge(ld_xl, 16 * (TILES // XG - EARLY))
                self_act(act, range(TILES))

            @block.tensor
            def _(pe):
                pe.wait_ge(consts, 5)
                pe.wait_ge(rows_f, 1)
                for a in range(2):
                    for b in range(ROWBLOCKS):
                        last = pe.transpose(bank[2 * a + b // 4][:, (b % 4) * P:(b % 4) * P + P], e_rowsf[:, a, b, :], ident[:])
                last.then_inc(rows_t, 1)
                def count(b, par, start, stop):
                    for c in range(HB):
                        last = pe.matmul(bank[4][:, 0:TILES], hot_lo[:, par, c, :], hot_hi[:, par, c, 0:TILES],
                                         start=start and c == 0, stop=stop and c == HB - 1, skip_group_check=True)
                    last.then_inc(counted, 1)
                pe.wait_ge(lo_built, HB - ACT_HB)
                pe.wait_ge(act_built, 1)
                pe.wait_ge(hi_built, 1)
                count(0, 0, True, False)
                with pe.Fori(0, (HBATCHES - 2) // HLOOP) as r:
                    for u in range(HLOOP):
                        pe.wait_ge(lo_built, r * (HLOOP * (HB - ACT_HB)) + (HB - ACT_HB) * (u + 2))
                        pe.wait_ge(act_built, r * HLOOP + u + 2)
                        pe.wait_ge(hi_built, r * HLOOP + u + 2)
                        count(None, 1 - u % 2, False, False)
                pe.wait_ge(lo_built, (HB - ACT_HB) * HBATCHES)
                pe.wait_ge(act_built, HBATCHES)
                pe.wait_ge(hi_built, HBATCHES)
                count(HBATCHES - 1, 1, False, True)
                pe.wait_ge(cnt_ready, 1)
                pe.matmul(bank[5][:, 0:TILES], ones, cnt, start=True, stop=True).then_inc(summed, 1)

            @block.vector
            def _(dve):
                done = [0]

                def link(i):
                    done[0] += 1
                    i.then_inc(chain0, 1)
                    dve.wait_ge(chain0, done[0])

                link(dve.memset(ones, 1.0))
                link(dve.memset(zeros, 0.0))
                link(dve.memset(biases.bitcast(F32), 0.0))
                dve.memset(ones_row.bitcast(F32), 0.0).then_inc(consts_v, 1)
                dve.wait_ge(consts_v, 1)
                dve.tensor_copy(ones_row[0:1], ones[0:1]).then_inc(consts_v, 1)
                link(dve.tensor_copy(ones_row[32:33], ones[32:33]))
                dve.wait_ge(ld_rows, 48)
                dve.tensor_copy(e_rowsf, e_rows[:, 0:2]).then_inc(rows_f, 1)
                link(dve.tensor_tensor(unsorted_at, e_rows[:, 1], e_rows[:, 2], ALU.is_gt))
                dve.tensor_reduce(unsorted, unsorted_at, AX.XY, ALU.max).then_inc(unsorted_rows, 1)
                dve.wait_ge(rows_t, 1)
                for a, to in ((0, edges[:, :, 0]), (1, i_all), (1, edges[:, :, 1].bitcast(F32))):
                    dve.tensor_copy(to[:, 0:4 * P], bank[2 * a][:]).then_inc(chain0, 1)
                    dve.tensor_copy(to[:, 4 * P:CHUNKS], bank[2 * a + 1][:, 0:CHUNKS - 4 * P]).then_inc(chain0, 1)
                    done[0] += 2
                dve.wait_ge(chain0, done[0])
                link(dve.tensor_scalar(i_lo, i_all, P - 1, None, ALU.bitwise_and))
                link(dve.tensor_scalar(i_hi, i_all, int(math.log2(P)), None, ALU.logical_shift_right))
                link(dve.tensor_copy(f_lo, i_lo))
                link(dve.tensor_copy(f_hi, i_hi))
                dve.sem_inc(lo_ready, 1)
                for w, w_in in enumerate((wq_in, wv_in)):
                    dve.wait_ge(w_hi, w + 1)
                    dve.tensor_tensor(w_split[:, w, 1], w_in, w_split[:, w, 0].bitcast(F32), ALU.subtract).then_inc(w_lo, 1)
                dve.wait_ge(w_lo, 2)
                dve.wait_ge(consts, 2)
                def hot_batch(b, par):
                    dve.tensor_tensor(hot_hi[:, par, :, 0:TILES],
                                      f_hi[:, bass.ds(b * HB, HB)].unsqueeze(2).to_broadcast([P, HB, TILES]),
                                      iota_row[:, 0:TILES].unsqueeze(1).to_broadcast([P, HB, TILES]),
                                      ALU.is_equal).then_inc(hi_built, 1)
                    for c in range(HB - ACT_HB):
                        dve.tensor_scalar(hot_lo[:, par, c, :], iota_bf, f_lo[:, bass.ds(b * HB + c, 1)], None,
                                          ALU.is_equal).then_inc(lo_built, 1)
                hot_batch(0, 0)
                hot_batch(1, 1)
                with dve.Fori(0, (HBATCHES - 2) // HLOOP) as r:
                    for u in range(HLOOP):
                        dve.wait_ge(counted, r * HLOOP + u + 1)
                        hot_batch(r * HLOOP + u + 2, u % 2)
                dve.wait_ge(counted, HBATCHES)
                dve.tensor_copy(cnt, bank[4][:, 0:TILES]).then_inc(cnt_ready, 1)
                dve.wait_ge(cnt_ready, 1)
                dve.wait_ge(consts, 6)
                link(dve.tensor_scalar(deg, cnt, 1.0, 1e-12, ALU.add, ALU.max))
                dve.sem_inc(deg_ready, 1)
                dve.wait_ge(b_hi, 2)
                link(dve.tensor_tensor(biases[32:33], b_in[32:33], biases[32:33].bitcast(F32), ALU.subtract))
                dve.wait_ge(summed, 1)
                link(dve.tensor_tensor_scan(cums, bank[5][:, 0:TILES], zeros, 0.0, ALU.add, ALU.add))
                link(dve.tensor_copy(cum_i, cums))
                link(dve.tensor_scalar(met_i, cum_i, int(math.log2(L)), None, ALU.logical_shift_right))
                link(dve.tensor_copy(rank, met_i))
                link(dve.tensor_tensor(rank[:, 0:TILES - 1], rank[:, 0:TILES - 1], iota_row[:, 1:TILES], ALU.add))
                link(dve.tensor_tensor(cmp_t, rank[:, 0:TILES - 1].unsqueeze(1).to_broadcast([P, TCOLS, TILES - 1]),
                                       step_no.unsqueeze(2).to_broadcast([P, TCOLS, TILES - 1]), ALU.is_le))
                link(dve.tensor_reduce(t_f, cmp_t, AX.X, ALU.add))
                link(dve.tensor_tensor(g_f, step_no, t_f, ALU.subtract))
                dve.tensor_copy(tab_i[:, 0, :], t_f).then_inc(table_ready, 1)
                dve.tensor_copy(tab_i[:, 1, :], g_f).then_inc(table_ready, 1)
                dve.wait_ge(unsorted_all, 1)
                link(dve.tensor_scalar(small[:, 2:3], small[:, 1:2], FAR, None, ALU.mult))
                dve.tensor_scalar(off_f, t_f, float(P), small[:, 2:3], ALU.mult, ALU.add).then_inc(table_ready, 1)
                dve.wait_ge(dinv_ready, 1)
                dve.wait_ge(ld_xe, 16 * EARLY)
                dve.wait_ge(ld_xl, 16 * (TILES // XG - EARLY))
                self_dve(dve, range(TILES))

        col_ready, gathered = sem("col_ready"), [sem(f"gathered{r}") for r in range(max(RINGS))]
        g_hi, g_lo, summed_up, added = sem("g_hi"), sem("g_lo"), sem("summed_up"), sem("added")
        rel_ready, distance, hot_ready = sem("rel_ready"), sem("distance"), sem("hot_ready")

        class Steps:

            def __init__(self, phase):
                self.n = PHASE_STEPS[phase]
                self.units = self.n * UNITS
                self.base = TILES * sum(PHASE_STEPS[:phase])
                self.ring = RINGS[phase]
                self.act_hot = ACT_HOT[phase]
                self.hots = sum(TILES * n * UNITS for n, a in zip(PHASE_STEPS[:phase], ACT_HOT) if a)
                assert 2 * self.units % self.ring == 0
                self.uses = [sum(len(range(b, TILES * n * UNITS, ring)) for n, ring in zip(PHASE_STEPS[:phase], RINGS)
                                 if b < ring) for b in range(max(RINGS))]

            def lows(self, u):
                first = self.base * UNITS
                before = first * 2 - self.hots
                return (u - first) * (1 if self.act_hot else 2) + before

            def step(self, off, pair, k):
                return self.base + off * self.n + k + pair * (2 * self.n)

            def unit(self, off, pair, j):
                c = off * self.units + j
                return self.base * UNITS + c + pair * (2 * self.units), c

            def value(self, engine, row, s, top):
                _, v = nc.values_load_multi_w_load_instructions(
                    tab[0:1, row, bass.ds(s, 1)], [engine], min_val=0, max_val=top)
                return v[0]

            def pool_turn(self, pool, off, pair):
                first = isinstance(pair, int) and off == 0
                last = isinstance(pair, int) and off == TILES - 1
                if first:
                    self.columns(pool, off, pair, 0)
                for j in range(self.units):
                    u, c = self.unit(off, pair, j)
                    slot = c % self.ring
                    if not (last and j == self.units - 1):
                        self.columns(pool, off, pair, j + 1)
                    pool.wait_ge(col_ready, u + 1)
                    apart(pool)
                    for k in range(K):
                        pool.indirect_dma_start(gath[:, slot, k * D:k * D + D], None, y_dram,
                                                bass.IndirectOffsetOnAxis(ap=stage[:, slot, k, 0:1], axis=0)
                                                ).then_inc(gathered[slot], 16)

            def columns(self, pool, off, pair, j):
                u, c = self.unit(off, pair, j)
                group = self.value(ENG.Pool, 1, self.step(off, pair, j), CHUNKS // K - 1)
                if not (isinstance(pair, int) and c < self.ring):
                    pool.wait_ge(g_lo, self.lows(u - self.ring + 1))
                    apart(pool)
                pool.tensor_copy(stage[:, c % self.ring], edges[:, bass.ds(group * K, K), :]).then_inc(col_ready, 1)

            def act_unit(self, act, off, pair, j):
                u, c = self.unit(off, pair, j)
                slot = c % self.ring
                act.wait_ge(gathered[slot], (self.uses[slot] + c // self.ring + 1 + pair * (2 * self.units // self.ring)) * (16 * K))
                if not (isinstance(pair, int) and c < 2):
                    act.wait_ge(summed_up, u - 1)
                act.activation(g_hl[:, c % 2, 0], gath[:, slot], ACT.Copy).then_inc(g_hi, 1)
                if not self.act_hot:
                    return
                h = u - self.base * UNITS + self.hots
                if isinstance(pair, int) and c == 0:
                    self.distances(act, h, c)
                act.wait_ge(distance, (h + 1) * K)
                act.activation(onehot[:, c % 2], dist, ACT.Relu, bias=1.0, scale=-1.0).then_inc(hot_ready, 1)
                if not (isinstance(pair, int) and c == TILES * self.units - 1):
                    self.distances(act, h + 1, c + 1)

            def distances(self, act, h, c):
                act.wait_ge(rel_ready, h + 1)
                wait(act, hot_ready, h)
                for k in range(K):
                    act.activation(dist[:, k, :], iota_row[:], ACT.Abs, bias=dst_rel[:, c % 2, k:k + 1],
                                   scale=-1.0).then_inc(distance, 1)

            def relative(self, dve, s, u, c):
                h = u - self.base * UNITS + self.hots
                dve.wait_ge(col_ready, u + 1)
                wait(dve, distance, (h - 1) * K)
                dve.tensor_scalar(dst_rel[:, c % 2], stage[:, c % self.ring, :, 1].bitcast(F32), off_t[:, bass.ds(s, 1)],
                                  None, ALU.subtract).then_inc(rel_ready, 1)

            def dve_unit(self, dve, off, pair, j):
                u, c = self.unit(off, pair, j)
                slot = c % self.ring
                s = self.step(off, pair, j // UNITS)
                if self.act_hot:
                    if isinstance(pair, int) and c == 0:
                        self.relative(dve, s, u, c)
                    if not (isinstance(pair, int) and c == TILES * self.units - 1):
                        self.relative(dve, s + 1, u + 1, c + 1)
                else:
                    dve.wait_ge(col_ready, u + 1)
                if not (isinstance(pair, int) and c < 2):
                    dve.wait_ge(summed_up, u - 1)
                if not self.act_hot:
                    dve.scalar_tensor_tensor(onehot[:, c % 2], iota_row[:, None, :].to_broadcast([P, K, P]), off_t[:, bass.ds(s, 1)],
                                             stage[:, slot, :, 1:2].bitcast(F32).to_broadcast([P, K, P]),
                                             ALU.add, ALU.is_equal).then_inc(g_lo, 1)
                dve.wait_ge(g_hi, u + 1)
                dve.tensor_tensor(g_hl[:, c % 2, 1], gath[:, slot], g_hl[:, c % 2, 0].bitcast(F32),
                                  ALU.subtract).then_inc(g_lo, 1)
                if j % UNITS == 0 and c > 0:
                    self.add(dve, s - 1, (c // UNITS - 1) % 2)

            def add(self, dve, s, half):
                t = self.value(ENG.DVE, 0, s, TILES - 1)
                dve.wait_ge(summed_up, (s + 1) * UNITS)
                if not (isinstance(s, int) and s == 0):
                    dve.wait_ge(added, s)
                dve.tensor_tensor(row_tile(acc, t), row_tile(acc, t), agg_bank[half][:], ALU.add).then_inc(added, 1)

            def dve_last(self, dve):
                s = self.base + TILES * self.n - 1
                self.add(dve, s, (TILES * self.n - 1) % 2)

            def pe_unit(self, pe, off, pair, j):
                u, c = self.unit(off, pair, j)
                if self.act_hot:
                    pe.wait_ge(hot_ready, u + 1 - self.base * UNITS + self.hots)
                pe.wait_ge(g_lo, self.lows(u + 1))
                if j % UNITS == 0 and not (isinstance(pair, int) and c < 2 * UNITS):
                    pe.wait_ge(added, self.step(off, pair, j // UNITS) - 1)
                for k in range(K):
                    for h in range(2):
                        last = pe.matmul(agg_bank[c // UNITS % 2][:], onehot[:, c % 2, k, :], g_hl[:, c % 2, h, k * D:k * D + D],
                                         start=j % UNITS == 0 and k == 0 and h == 0,
                                         stop=j % UNITS == UNITS - 1 and k == K - 1 and h == 1)
                last.then_inc(summed_up, 1)

        def row_tile(a, i):
            return a[:, bass.ds(i, 1), :].rearrange("p a d -> p (a d)")

        def for_turns2(eng, turn, lag):
            for i in range(3):
                turn(i, 0)
            with eng.Fori(1, (TILES - 3) // 2) as r:
                turn(1, r)
                turn(2, r)
            for i in range(TILES - 2, TILES + lag):
                turn(i, 0)

        def has2(off, pair, lag):
            return not isinstance(pair, int) or 0 <= off - lag < TILES

        def wait(eng, semaphore, value):
            if not (isinstance(value, int) and value <= 0):
                eng.wait_ge(semaphore, value)

        x_loaded, v_stored = sem("x_loaded"), sem("v_stored")
        x_turned, x_hi, x_lo = sem("x_turned"), sem("x_hi"), sem("x_lo")
        q_mul, v_mul, q_relu, q_stat, q_done, v_done = (
            sem("q_mul"), sem("v_mul"), sem("q_relu"), sem("q_stat"), sem("q_done"), sem("v_done"))
        q_stored = [sem(f"q_stored{b}") for b in range(2)]
        steps1 = Steps(0)
        q_sq = sem("q_sq")
        q_sum = small[:, 14:16]
        neg_mean = small[:, 16:18]

        with nc.Block() as block:
            @block.sync
            def _(sp):
                def turn(off, pair):
                    i, par = off + pair * 2, off % 2
                    if has2(off, pair, 0):
                        wait(sp, x_turned, i)
                        sp.dma_start(x_in, row_tile(x_r, i)).then_inc(x_loaded, 16)
                    if has2(off, pair, 2):
                        sp.wait_ge(v_done, i - 1)
                        sp.dma_start(row_tile(v_r, i - 2), v_out).then_inc(v_stored, 16)
                    if has2(off, pair, 3):
                        sp.wait_ge(q_done, i - 2)
                        sp.dma_start(row_tile(q_r, i - 3), q_out[:, 1 - par]).then_inc(q_stored[1 - par], 16)
                for_turns2(sp, turn, 3)
                sp.wait_ge(v_stored, 16 * TILES)
                for b in range(2):
                    sp.wait_ge(q_stored[b], 16 * ((TILES + 1 - b) // 2))

            @block.gpsimd
            def _(pool):
                pool.wait_ge(y_stored, 16 * (TILES // XG))
                for_turns2(pool, lambda off, pair: steps1.pool_turn(pool, off, pair), 0)

            @block.scalar
            def _(act):
                def turn(off, pair):
                    i, par = off + pair * 2, off % 2
                    for j in range(steps1.units):
                        if has2(off, pair, 0):
                            steps1.act_unit(act, off, pair, j)
                        if j == 0 and has2(off, pair, 2):
                            act.wait_ge(v_mul, i - 1)
                            wait(act, v_stored, (i - 2) * 16)
                            act.activation(v_out, bank[2][:], ACT.Copy).then_inc(v_done, 1)
                        if j == 2 and has2(off, pair, 2):
                            act.wait_ge(q_stat, i - 1)
                            act.activation(bank[3][:], q_out[:, par], ACT.Square, bias=neg_mean[:, par:par + 1],
                                           accum_out=var_q[:, bass.ds(i - 2, 1)]).then_inc(q_sq, 1)
                            act.wait_ge(q_sq, i - 1)
                            act.activation(q_out[:, par], q_out[:, par], ACT.Relu, bias=neg_mean[:, par:par + 1],
                                           accum_out=s0[:, bass.ds(i - 2, 1)]).then_inc(q_done, 1)
                        if j == 3 and has2(off, pair, 0):
                            act.wait_ge(x_turned, i + 1)
                            wait(act, v_mul, i - 1)
                            act.activation(x_hl[:, par, 0], bank[0][:], ACT.Copy).then_inc(x_hi, 1)
                        if j == 3 and has2(off, pair, 1):
                            act.wait_ge(q_mul, i)
                            b = 1 - par
                            wait(act, q_stored[b], (pair + (off - 1) // 2) * 16)
                            act.activation(q_out[:, b], bank[1][:], ACT.Relu, accum_out=q_sum[:, b:b + 1]).then_inc(q_relu, 1)
                for_turns2(act, turn, 2)

            @block.tensor
            def _(pe):
                def project(w, part, par):
                    dest = bank[1 + w]
                    if part == 0:
                        pe.matmul(dest[:], ones_row, biases[:, w, :], start=True, stop=False)
                    for c in range(KD // 2 * part, KD // 2 * (part + 1)):
                        for a, b in ((0, 0), (0, 1), (1, 0)):
                            last = pe.matmul(dest[:], x_hl[:, par, a, c * P:c * P + P], w_split[:, w, b, c, :],
                                             start=False, stop=c == KD - 1 and a == 1)
                    if part == 1:
                        last.then_inc((q_mul, v_mul)[w], 1)

                def turn(off, pair):
                    i, par = off + pair * 2, off % 2
                    for j in range(steps1.units):
                        if has2(off, pair, 0):
                            steps1.pe_unit(pe, off, pair, j)
                        if j < 4 and has2(off, pair, 1):
                            if j == 0:
                                pe.wait_ge(x_lo, i)
                                wait(pe, q_relu, i - 1)
                            if j == 2:
                                wait(pe, v_done, i - 1)
                            project(j // 2, j % 2, 1 - par)
                        if j == 1 and has2(off, pair, 0):
                            pe.wait_ge(x_loaded, (i + 1) * 16)
                            wait(pe, x_lo, i)
                            for c in range(KD):
                                last = pe.transpose(bank[0][:, c * P:c * P + P], x_in[:, c * P:c * P + P], ident[:])
                            last.then_inc(x_turned, 1)
                for_turns2(pe, turn, 1)

            @block.vector
            def _(dve):
                dve.wait_ge(y_stored, 16 * (TILES // XG))
                def turn(off, pair):
                    i, par = off + pair * 2, off % 2
                    for j in range(steps1.units):
                        if has2(off, pair, 0):
                            steps1.dve_unit(dve, off, pair, j)
                        if j == 1 and has2(off, pair, 2):
                            m = i - 2
                            dve.wait_ge(q_relu, m + 1)
                            wait(dve, q_done, m - 1)
                            dve.tensor_scalar(neg_mean[:, par:par + 1], q_sum[:, par:par + 1], -1.0 / D, None, ALU.mult
                                              ).then_inc(q_stat, 1)
                        if j == 3 and has2(off, pair, 0):
                            dve.wait_ge(x_hi, i + 1)
                            wait(dve, v_mul, i - 1)
                            dve.tensor_tensor(x_hl[:, par, 1], bank[0][:], x_hl[:, par, 0].bitcast(F32), ALU.subtract).then_inc(x_lo, 1)
                for_turns2(dve, turn, 2)
                steps1.dve_last(dve)

        chain1, rstd_ready, extremes, angles, valid_ready = (
            sem("chain1"), sem("rstd_ready"), sem("extremes"), sem("angles"), sem("valid_ready"))
        sines = sem("sines")
        scr = f_pool[:, 4096:4096 + 16 * 64].rearrange("p (n t) -> p n t", t=64)
        var_eps, halves, node_no, valid, rs, h2, hang, turns, r1, r2, r3, sin_in, trig, hmm = (
            scr[:, n, 0:TILES] for n in range(14))
        ext = small[:, 20:22]
        ext_all = small[:, 22:24]
        mfac = small[:, 24:28]
        TWO_PI = 2 * math.pi
        PI_A = 6.28125
        PI_B = float(int((TWO_PI - PI_A) * 2**21) / 2**21)
        PI_C = TWO_PI - PI_A - PI_B
        ROUND = 1.5 * 2**23

        with nc.Block() as block:
            @block.gpsimd
            def _(pool):
                pool.iota(node_no, [[P, TILES]], base=0, channel_multiplier=1,
                          allow_small_or_imprecise_dtypes=True).then_inc(valid_ready, 1)
                pool.memset(halves, -0.5).then_inc(valid_ready, 1)
                pool.wait_ge(valid_ready, 2)
                pool.wait_ge(rstd_ready, 1)
                pool.tensor_tensor(rstd[:], var_eps, halves, ALU.pow).then_inc(rstd_ready, 1)
                pool.wait_ge(extremes, 1)
                pool.partition_all_reduce(ext_all, ext, P, bass.bass_isa.ReduceOp.max).then_inc(extremes, 1)

            @block.vector
            def _(dve):
                done = [0]

                def link(i):
                    done[0] += 1
                    i.then_inc(chain1, 1)
                    dve.wait_ge(chain1, done[0])

                dve.tensor_scalar(var_eps, var_q[:, 0:TILES], 1.0 / D, EPS_LN, ALU.mult, ALU.add).then_inc(rstd_ready, 1)
                dve.wait_ge(valid_ready, 1)
                link(dve.tensor_scalar(valid, node_no, float(N), None, ALU.is_lt))
                dve.wait_ge(rstd_ready, 2)
                link(dve.tensor_tensor(rs, rstd[:], s0[:], ALU.mult))
                link(dve.tensor_tensor(h2, rs, rs, ALU.mult))
                link(dve.tensor_tensor(hmm, h2, valid, ALU.mult))
                link(dve.tensor_reduce(ext[:, 0:1], hmm, AX.X, ALU.max))
                link(dve.tensor_scalar(r1, valid, 1.0, -3e38, ALU.subtract, ALU.mult))
                link(dve.tensor_tensor(r2, hmm, r1, ALU.add))
                link(dve.tensor_reduce(r3[:, 0:1], r2, AX.X, ALU.min))
                dve.tensor_scalar(ext[:, 1:2], r3[:, 0:1], -1.0, None, ALU.mult).then_inc(extremes, 1)
                dve.wait_ge(extremes, 2)
                link(dve.tensor_tensor(mfac[:, 0:1], ext_all[:, 0:1], ext_all[:, 1:2], ALU.add))
                link(dve.tensor_scalar(mfac[:, 1:2], mfac[:, 0:1], 4.0, None, ALU.mult))
                link(dve.reciprocal(mfac[:, 2:3], mfac[:, 1:2]))
                link(dve.tensor_scalar(mfac[:, 3:4], mfac[:, 2:3], math.pi, None, ALU.mult))
                link(dve.tensor_scalar(hang, h2, mfac[:, 3:4], None, ALU.mult))
                for f, shift in enumerate((0.25, 0.0)):
                    link(dve.tensor_scalar(turns, hang, 1 / TWO_PI, shift, ALU.mult, ALU.add))
                    link(dve.tensor_scalar(r1, turns, ROUND, None, ALU.add))
                    link(dve.tensor_scalar(turns, r1, -ROUND, None, ALU.add))
                    link(dve.scalar_tensor_tensor(r1, turns, -PI_A, hang, ALU.mult, ALU.add))
                    link(dve.scalar_tensor_tensor(r2, turns, -PI_B, r1, ALU.mult, ALU.add))
                    link(dve.scalar_tensor_tensor(r3, turns, -PI_C, r2, ALU.mult, ALU.add))
                    link(dve.tensor_scalar(r1, r3, shift * TWO_PI, math.pi, ALU.add, ALU.min))
                    dve.tensor_scalar(sin_in, r1, -math.pi, None, ALU.max).then_inc(angles, 1)
                    dve.wait_ge(sines, f + 1)
                    link(dve.tensor_tensor(r1, trig, rstd[:], ALU.mult))
                    link(dve.tensor_tensor(r2, r1, valid, ALU.mult))
                    link(dve.tensor_copy(cs[:, :, 2 * f], r2))
                    link(dve.tensor_copy(cs[:, :, 2 * f + 1], r2))
                    link(dve.tensor_copy(cs_split[:, :, f, 0], r2))
                    link(dve.tensor_tensor(cs_split[:, :, f, 1], r2, cs_split[:, :, f, 0].bitcast(F32), ALU.subtract))

            @block.scalar
            def _(act):
                for f in range(2):
                    act.wait_ge(angles, f + 1)
                    act.activation(trig, sin_in, ACT.Sin).then_inc(sines, 1)

        for f in range(2):
            qv_loaded = [sem(f"qv_loaded{f}{b}") for b in range(2)]
            q_hi, v_hi, qv_lo, kv_mul = sem(f"q_hi{f}"), sem(f"v_hi{f}"), sem(f"qv_lo{f}"), sem(f"kv_mul{f}")
            kv_hi, kv_lo = sem(f"kv_hi{f}"), sem(f"kv_lo{f}")
            steps2 = Steps(1 + f)

            with nc.Block() as block:
                @block.sync
                def _(sp, qv_loaded=qv_loaded, qv_lo=qv_lo):
                    def turn(off, pair):
                        i, par = off + pair * 2, off % 2
                        wait(sp, qv_lo, (i - 1) * 2)
                        for w, a in enumerate((q_r, v_r)):
                            sp.dma_start(qv_in[:, par, w], row_tile(a, i)).then_inc(qv_loaded[par], 16)
                    for_turns2(sp, turn, 0)

                @block.gpsimd
                def _(pool, steps2=steps2):
                    for_turns2(pool, lambda off, pair: steps2.pool_turn(pool, off, pair), 0)

                @block.scalar
                def _(act, f=f, steps2=steps2, qv_loaded=qv_loaded, q_hi=q_hi, v_hi=v_hi, kv_mul=kv_mul, kv_hi=kv_hi):
                    def turn(off, pair):
                        i, par = off + pair * 2, off % 2
                        for j in range(steps2.units):
                            steps2.act_unit(act, off, pair, j)
                        act.wait_ge(qv_loaded[par], (off // 2 + pair + 1) * 32)
                        wait(act, kv_mul, i - 1)
                        act.activation(qv_hl[:, par, 0, 0], qv_in[:, par, 0], ACT.Copy).then_inc(q_hi, 1)
                        act.activation(qv_hl[:, par, 1, 0], qv_in[:, par, 1], ACT.Copy,
                                       scale=cs[:, bass.ds(i, 1), 2 * f]).then_inc(v_hi, 1)
                    for_turns2(act, turn, 0)
                    act.wait_ge(kv_mul, TILES)
                    for c in range(KD):
                        act.activation(w_split[:, f, 0, c, :], bank[c][:], ACT.Copy).then_inc(kv_hi, 1)

                @block.tensor
                def _(pe, f=f, steps2=steps2, qv_lo=qv_lo, kv_mul=kv_mul):
                    def turn(off, pair):
                        i, par = off + pair * 2, off % 2
                        if has2(off, pair, 1):
                            first = isinstance(pair, int) and off == 1
                            pe.wait_ge(qv_lo, i * 2)
                        share = KD // steps2.units if steps2.units < KD else 1
                        for j in range(max(steps2.units, KD)):
                            if j < steps2.units and has2(off, pair, 0):
                                steps2.pe_unit(pe, off, pair, j)
                            if not has2(off, pair, 1):
                                continue
                            for c in range(j * share, min(KD, (j + 1) * share)):
                                for a, b in ((0, 0), (0, 1), (1, 0)):
                                    q = qv_hl[:, 1 - par, 0, a, c * P:c * P + P]
                                    pe.matmul(bank[c][:], q, qv_hl[:, 1 - par, 1, b], start=first and a == 0 and b == 0,
                                              stop=True, skip_group_check=True)
                                    if b == 0:
                                        last = pe.matmul(bank[4][:, 2 * c:2 * c + 2], q,
                                                         cs_split[:, bass.ds(i - 1, 1), f, :].rearrange("p a b -> p (a b)"),
                                                         start=first and c == 0 and a == 0, stop=True, skip_group_check=True)
                                if c == KD - 1:
                                    last.then_inc(kv_mul, 1)
                    for_turns2(pe, turn, 1)

                @block.vector
                def _(dve, f=f, steps2=steps2, q_hi=q_hi, v_hi=v_hi, qv_lo=qv_lo, kv_mul=kv_mul, kv_hi=kv_hi, kv_lo=kv_lo):
                    def turn(off, pair):
                        i, par = off + pair * 2, off % 2
                        for j in range(steps2.units):
                            steps2.dve_unit(dve, off, pair, j)
                        dve.wait_ge(q_hi, i + 1)
                        dve.tensor_tensor(qv_hl[:, par, 0, 1], qv_in[:, par, 0], qv_hl[:, par, 0, 0].bitcast(F32),
                                          ALU.subtract).then_inc(qv_lo, 1)
                        dve.wait_ge(v_hi, i + 1)
                        dve.scalar_tensor_tensor(qv_hl[:, par, 1, 1], qv_in[:, par, 1], cs[:, bass.ds(i, 1), 2 * f],
                                                 qv_hl[:, par, 1, 0].bitcast(F32), ALU.mult, ALU.subtract).then_inc(qv_lo, 1)
                    for_turns2(dve, turn, 0)
                    steps2.dve_last(dve)
                    for c in range(KD):
                        dve.wait_ge(kv_hi, c + 1)
                        dve.tensor_tensor(w_split[:, f, 1, c, :], bank[c][:], w_split[:, f, 0, c, :].bitcast(F32),
                                          ALU.subtract).then_inc(kv_lo, 1)
                    dve.tensor_reduce(q_col[:, f], bank[4][:, 0:2 * KD].rearrange("p (c h) -> p c h", h=2), AX.X, ALU.add
                                      ).then_inc(kv_lo, 1)

        x2 = f_pool[:, 0:1024].rearrange("p (s d) -> p s d", s=2)
        q_sums = f_pool[:, 1024:2048].rearrange("p (f d) -> p f d", f=2)
        q2 = f_pool[:, 2048:3072].rearrange("p (s d) -> p s d", s=2)
        v2 = f_pool[:, 3072:4096].rearrange("p (s d) -> p s d", s=2)
        u2 = f_pool[:, 4096:5120].rearrange("p (s d) -> p s d", s=2)
        t4 = f_pool[:, 5120:7168].rearrange("p (s d) -> p s d", s=4)
        wg_in = f_pool[:, 5120:7168].rearrange("p (c d) -> p c d", c=KD)
        affine = edges[:].rearrange("p c w -> p (c w)")[:, 0:3 * D].bitcast(F32).rearrange("p (a d) -> p a d", a=3)
        z2 = tables[:, 0:2 * D].bitcast(F32).rearrange("p (s d) -> p s d", s=2)
        st1 = small[:, 0:32].rearrange("p (s c) -> p s c", s=2)
        st2 = small[:, 32:64].rearrange("p (s c) -> p s c", s=2)
        nrm = var_q[:, 0:32].rearrange("p (s c) -> p s c", s=2)

        expo = var_q[:, 40:41]

        ld3, wg_hi_done, wg_lo_done, expo_ready = sem("ld3"), sem("wg_hi_done"), sem("wg_lo_done"), sem("expo_ready")
        x3_loaded = [sem(f"x3_loaded{b}") for b in range(2)]
        spread, q_sums_ready = sem("spread"), sem("q_sums_ready")
        q3_loaded = [sem(f"q3_loaded{b}") for b in range(2)]
        v3_loaded = [sem(f"v3_loaded{b}") for b in range(2)]
        out_stored = [sem(f"out_stored{b}") for b in range(4)]
        z_made = sem("z_made")
        turned, t_hi, t_lo = sem("turned"), sem("t_hi"), sem("t_lo")
        mul_a, mul_b, mul_c = sem("mul_a"), sem("mul_b"), sem("mul_c")
        vb, norms, u_a, u_sum, stat1, stat2 = (
            sem("vb"), sem("norms"), sem("u_a"), sem("u_sum"), sem("stat1"), sem("stat2"))
        rstd1, rstd2, shift1, shift2 = sem("rstd1"), sem("rstd2"), sem("shift1"), sem("shift2")
        normed, scaled, residual, out_done = sem("normed"), sem("scaled"), sem("residual"), sem("out_done")

        def for_turns(eng, body):
            for i in range(6):
                body(i, i // 4, i % 4)
            with eng.Fori(1, (TILES - 2) // 4) as r:
                for n in range(2, 6):
                    body(r * 4 + n, r + n // 4, n % 4)
            for i in range((TILES - 2) // 4 * 4 + 2, TILES + 3):
                body(i, i // 4, i % 4)

        def has(i, lag):
            return not isinstance(i, int) or 0 <= i - lag < TILES

        def after(eng, i, first, semaphore, value):
            if not (isinstance(i, int) and i < first):
                eng.wait_ge(semaphore, value)

        with nc.Block() as block:
            @block.sync
            def _(sp):
                sp.dma_start(wg_in, Wg.rearrange("(c p) d -> p c d", p=P)).then_inc(ld3, 16)
                for n, b in enumerate((gamma, beta, bg)):
                    sp.dma_start(affine[:, n], b[None, :].to_broadcast([P, D])).then_inc(ld3, 16)

                def turn(i, r, n):
                    if has(i, 0):
                        after(sp, i, 2, turned, i - 1)
                        after(sp, i, 2, norms, i * 6 - 9)
                        sp.dma_start(q2[:, n % 2], row_tile(q_r, i)).then_inc(q3_loaded[n % 2], 16)
                        after(sp, i, 2, u_sum, (i - 1) * 3)
                        sp.dma_start(v2[:, n % 2], row_tile(v_r, i)).then_inc(v3_loaded[n % 2], 16)
                    if has(i, 2):
                        after(sp, i, 4, residual, i - 3)
                        sp.dma_start(x2[:, n % 2], row_tile(x_r, i - 2)).then_inc(x3_loaded[n % 2], 16)
                    if has(i, 4):
                        sp.wait_ge(out_done, i - 3)
                        sp.dma_start(row_tile(out_r, i - 4), t4[:, n]).then_inc(out_stored[n], 16)
                for_turns(sp, turn)
                sp.wait_ge(out_done, TILES)
                sp.dma_start(row_tile(out_r, TILES - 1), t4[:, (TILES - 1) % 4]).then_inc(out_stored[(TILES - 1) % 4], 16)
                for b in range(4):
                    sp.wait_ge(out_stored[b], 16 * len(range(b, TILES, 4)))

            @block.gpsimd
            def _(pool):
                pool.memset(expo, -0.5).then_inc(expo_ready, 1)
                pool.wait_ge(expo_ready, 1)
                pool.wait_ge(ld3, 64)

                def power(i, lag, stat, st, ready):
                    pool.wait_ge(stat, (i - lag + 1) * 2)
                    apart(pool)
                    pool.tensor_scalar(st[:, 8:9], st[:, 7:8], EPS_LN, None, ALU.add).then_inc(ready, 1)
                    pool.wait_ge(ready, (i - lag) * 2 + 1)
                    pool.tensor_tensor(st[:, 8:9], st[:, 8:9], expo, ALU.pow).then_inc(ready, 1)

                def scale_row(i, n):
                    apart(pool)
                    pool.tensor_tensor(z2[:, n % 2], row_tile(acc, i), dinv[:, bass.ds(i, 1)].to_broadcast([P, D]),
                                       ALU.mult).then_inc(z_made, 1)

                scale_row(0, 0)

                def turn(i, r, n):
                    if has(i, -1):
                        after(pool, i, 1, turned, i)
                        scale_row(i + 1, n + 1)
                    if has(i, 0):
                        pool.wait_ge(v3_loaded[n % 2], (r * 2 + n // 2 + 1) * 16)
                        pool.tensor_tensor(v2[:, n % 2], v2[:, n % 2], affine[:, 2], ALU.add).then_inc(vb, 1)
                    if has(i, 3):
                        power(i, 3, stat2, st2[:, (n - 3) % 2], rstd2)
                    if has(i, 2):
                        t = t4[:, (n - 2) % 4]
                        pool.wait_ge(normed, i - 1)
                        pool.tensor_tensor(t, t, affine[:, 0], ALU.mult).then_inc(scaled, 1)
                        pool.wait_ge(scaled, (i - 2) * 2 + 1)
                        pool.tensor_tensor(t, t, affine[:, 1], ALU.add).then_inc(scaled, 1)
                    if has(i, 1):
                        power(i, 1, stat1, st1[:, (n - 1) % 2], rstd1)
                for_turns(pool, turn)

            @block.scalar
            def _(act):
                def turn(i, r, n):
                    if isinstance(i, int) and i == 1:
                        act.wait_ge(ld3, 64)
                        act.activation(wg_hl[:, 0], wg_in, ACT.Copy).then_inc(wg_hi_done, 1)
                    if has(i, 0):
                        act.wait_ge(turned, i + 1)
                        after(act, i, 2, mul_c, i - 1)
                        for w in range(2):
                            act.activation(qz_hl[:, n % 2, w, 0], bank[w][:], ACT.Copy).then_inc(t_hi, 1)
                    if has(i, 2):
                        b = (n - 2) % 4
                        if isinstance(i, int) and i == 2:
                            act.wait_ge(wg_lo_done, 1)
                        act.wait_ge(shift1, i - 1)
                        after(act, i, 6, out_stored[b], (r + (n - 2) // 4) * 16)
                        s = st1[:, n % 2]
                        act.activation(t4[:, b], u2[:, n % 2], ACT.Identity, bias=s[:, 9:10], scale=s[:, 8:9]).then_inc(normed, 1)
                    if has(i, 1):
                        act.wait_ge(mul_a, i)
                        act.wait_ge(norms, i * 6)
                        after(act, i, 3, normed, i - 2)
                        act.activation(u2[:, (n - 1) % 2], bank[2][:], ACT.Copy, scale=nrm[:, (n - 1) % 2, 6:7]).then_inc(u_a, 1)
                    if has(i, 3):
                        act.wait_ge(shift2, i - 2)
                        s = st2[:, (n - 3) % 2]
                        t = t4[:, (n - 3) % 4]
                        act.activation(t, t, ACT.Identity, bias=s[:, 9:10], scale=s[:, 8:9]).then_inc(out_done, 1)
                for_turns(act, turn)

            @block.tensor
            def _(pe):
                def turn(i, r, n):
                    if has(i, 0):
                        pe.wait_ge(q3_loaded[n % 2], (r * 2 + n // 2 + 1) * 16)
                        after(pe, i, 1, t_lo, i * 2)
                        for c in range(KD):
                            pe.transpose(bank[0][:, c * P:c * P + P], q2[:, n % 2, c * P:c * P + P], ident[:])
                        pe.wait_ge(z_made, i + 1)
                        for c in range(KD):
                            last = pe.transpose(bank[1][:, c * P:c * P + P], z2[:, n % 2, c * P:c * P + P], ident[:])
                        last.then_inc(turned, 1)
                    if has(i, 1):
                        pe.wait_ge(t_lo, i * 2)
                        qz = qz_hl[:, (n - 1) % 2]
                        def product(dest, w, weight, mul):
                            for c in range(KD):
                                for a, b in ((0, 0), (0, 1), (1, 0)):
                                    last = pe.matmul(dest[:], qz[:, w, a, c * P:c * P + P], weight(b, c),
                                                     start=c == 0 and a == 0 and b == 0, stop=c == KD - 1 and a == 1)
                            last.then_inc(mul, 1)
                        after(pe, i, 2, u_a, i - 1)
                        product(bank[2], 0, lambda b, c: w_split[:, 0, b, c, :], mul_a)
                        after(pe, i, 2, u_sum, i * 3 - 5)
                        product(bank[3], 0, lambda b, c: w_split[:, 1, b, c, :], mul_b)
                        after(pe, i, 2, u_sum, i * 3 - 4)
                        if isinstance(i, int) and i == 1:
                            pe.wait_ge(wg_lo_done, 1)
                        product(bank[4], 1, lambda b, c: wg_hl[:, b, c, :], mul_c)
                for f in range(2):
                    for c in range(KD):
                        last = pe.matmul(bank[6 + f][:, c * P:c * P + P], q_col[:, f, c:c + 1].to_broadcast([P, P]), ident[:],
                                         start=True, stop=True)
                last.then_inc(spread, 1)
                for_turns(pe, turn)

            @block.vector
            def _(dve):
                def shift(st, rstd_sem, count, ready):
                    dve.wait_ge(rstd_sem, count)
                    dve.scalar_tensor_tensor(st[:, 9:10], st[:, 6:7], -1.0, st[:, 8:9], ALU.mult, ALU.mult).then_inc(ready, 1)

                def stats(st, a, stat, before):
                    dve.bn_stats(st[:, 0:6], a).then_inc(stat, 1)
                    dve.wait_ge(stat, before + 1)
                    apart(dve)
                    dve.bn_aggr(st[:, 6:8], st[:, 0:6]).then_inc(stat, 1)

                def turn(i, r, n):
                    if isinstance(i, int) and i == 1:
                        dve.wait_ge(wg_hi_done, 1)
                        dve.tensor_tensor(wg_hl[:, 1], wg_in, wg_hl[:, 0].bitcast(F32), ALU.subtract).then_inc(wg_lo_done, 1)
                    if isinstance(i, int) and i == 0:
                        dve.wait_ge(spread, 1)
                        for f in range(2):
                            dve.tensor_copy(q_sums[:, f], bank[6 + f][:]).then_inc(q_sums_ready, 1)
                        dve.wait_ge(q_sums_ready, 2)
                    if has(i, 0):
                        for w in range(2):
                            dve.wait_ge(t_hi, i * 2 + w + 1)
                            dve.tensor_tensor(qz_hl[:, n % 2, w, 1], bank[w][:], qz_hl[:, n % 2, w, 0].bitcast(F32),
                                              ALU.subtract).then_inc(t_lo, 1)
                    if has(i, 2):
                        shift(st1[:, n % 2], rstd1, (i - 1) * 2, shift1)
                    if has(i, 0):
                        s = nrm[:, n % 2]
                        dve.tensor_copy(s[:, 8:12], cs[:, bass.ds(i, 1), :].rearrange("p a b -> p (a b)")).then_inc(norms, 1)
                        for f in range(2):
                            dve.wait_ge(norms, i * 6 + f + 1)
                            dve.tensor_tensor_reduce(bank[5][:], q2[:, n % 2], q_sums[:, f],
                                                     1.0, 0.0, ALU.mult, ALU.add, s[:, f:f + 1]).then_inc(norms, 1)
                        dve.wait_ge(norms, i * 6 + 3)
                        dve.tensor_tensor_reduce(s[:, 2:4], s[:, 0:2], s[:, 8:12:2],
                                                 1.0, EPS_NORM, ALU.mult, ALU.add, s[:, 4:5]).then_inc(norms, 1)
                        dve.wait_ge(norms, i * 6 + 4)
                        dve.reciprocal(s[:, 5:6], s[:, 4:5]).then_inc(norms, 1)
                        dve.wait_ge(norms, i * 6 + 5)
                        dve.tensor_scalar(s[:, 6:8], s[:, 8:12:2], s[:, 5:6], None, ALU.mult).then_inc(norms, 1)
                        dve.wait_ge(norms, i * 6 + 6)
                    if has(i, 3):
                        b = (n - 3) % 4
                        dve.wait_ge(scaled, (i - 2) * 2)
                        dve.wait_ge(x3_loaded[(n - 3) % 2], (r * 2 + (n - 3) // 2 + 1) * 16)
                        dve.scalar_tensor_tensor(t4[:, b], t4[:, b], 0.0, x2[:, (n - 3) % 2], ALU.max, ALU.add).then_inc(residual, 1)
                        dve.wait_ge(residual, i - 2)
                        stats(st2[:, (n - 3) % 2], t4[:, b], stat2, (i - 3) * 2)
                    if has(i, 1):
                        s = nrm[:, (n - 1) % 2]
                        u = u2[:, (n - 1) % 2]
                        m = i - 1
                        dve.wait_ge(u_a, i)
                        dve.wait_ge(mul_b, i)
                        dve.scalar_tensor_tensor(u, bank[3][:], s[:, 7:8], u, ALU.mult, ALU.add).then_inc(u_sum, 1)
                        if has(i, 3):
                            shift(st2[:, (n - 3) % 2], rstd2, (i - 2) * 2, shift2)
                        dve.wait_ge(mul_c, i)
                        dve.wait_ge(u_sum, m * 3 + 1)
                        dve.tensor_tensor(u, bank[4][:], u, ALU.add).then_inc(u_sum, 1)
                        dve.wait_ge(vb, i)
                        dve.wait_ge(u_sum, m * 3 + 2)
                        dve.tensor_tensor(u, u, v2[:, (n - 1) % 2], ALU.add).then_inc(u_sum, 1)
                        dve.wait_ge(u_sum, m * 3 + 3)
                        stats(st1[:, (n - 1) % 2], u, stat1, m * 2)
                    elif has(i, 3):
                        shift(st2[:, (n - 3) % 2], rstd2, (i - 2) * 2, shift2)
                for_turns(dve, turn)


def kernel(x, src, dst, L0_gnn_Wq, L0_gnn_bq, L0_gnn_Wv, L0_gnn_bv, L0_gnn_Wg, L0_gnn_bg, L0_gnn_gamma,
           L0_gnn_beta):
    import numpy as np
    import concourse.bacc as bacc
    from concourse.bass_utils import run_bass_kernel_spmd

    xp = np.zeros((NPAD, D), np.float32)
    xp[:N] = np.asarray(x)
    sp = np.zeros(EPAD, np.int32)
    sp[:E] = np.asarray(src)
    dp = np.full(EPAD + P, NPAD, np.int32)
    dp[:E] = np.asarray(dst)
    arrays = {"x": xp, "src": sp, "dst": dp, "Wq": L0_gnn_Wq, "bq": L0_gnn_bq, "Wv": L0_gnn_Wv, "bv": L0_gnn_bv,
              "Wg": L0_gnn_Wg, "bg": L0_gnn_bg, "gamma": L0_gnn_gamma, "beta": L0_gnn_beta}
    arrays = {f"in_{k}": np.ascontiguousarray(a) for k, a in arrays.items()}
    nc = bacc.Bacc("TRN2", target_bir_lowering=False, num_devices=1)
    aps = {k[3:]: nc.dram_tensor(k, a.shape, mybir.dt.from_np(a.dtype), kind="ExternalInput").ap()
           for k, a in arrays.items()}
    out = nc.dram_tensor("out_0", (NPAD, D), F32, kind="ExternalOutput").ap()
    build(nc, out=out, **aps)
    r = run_bass_kernel_spmd(nc, [arrays], core_ids=[0])
    return r.results[0]["out_0"][:N]
```

```python
import math
from contextlib import ExitStack

import concourse.bass as bass
from concourse import mybir

F32 = mybir.dt.float32
F32R = mybir.dt.float32r
I32 = mybir.dt.int32
ALU = mybir.AluOpType
ACT = mybir.ActivationFunctionType
AX = mybir.AxisListType
ENG = mybir.EngineType

P = 128
N = 6250
D = 512
E = 100000
EPS_LN = 1e-5
EPS_NORM = 1e-10
TILES = -(-N // P)
NPAD = TILES * P
KD = D // P
K = 2
L = K * P
GROUPS = -(-E // L)
PHASE_STEPS = (5, 2, 2)
STEPS = TILES * sum(PHASE_STEPS)
assert STEPS >= GROUPS + TILES - 1
ACT_HOT = (False, True, True)
RINGS = (5, 4, 4)
ROWBLOCKS = -(-(STEPS - TILES + 1) * K // P)
CHUNKS = ROWBLOCKS * P
EPAD = CHUNKS * P
W = 512
assert W % P == 0 and EPAD % W == 0
TCOLS = -(-STEPS // P)


def build(nc, x, src, dst, Wq, bq, Wv, bv, Wg, bg, gamma, beta, out):
    with ExitStack() as ctx:
        def sb(name, shape, dt):
            return ctx.enter_context(nc.sbuf_tensor("sb_" + name, shape, dt))

        def sem(name):
            return ctx.enter_context(nc.semaphore(name))

        y_dram = nc.dram_tensor("y_scratch", [NPAD, D], F32).ap()
        q_dram = nc.dram_tensor("q_scratch", [NPAD, D], F32).ap()
        v_dram = nc.dram_tensor("v_scratch", [NPAD, D], F32).ap()
        tab_dram = nc.dram_tensor("tab_scratch", [2, TCOLS * P], I32).ap()
        off_dram = nc.dram_tensor("off_scratch", [1, TCOLS * P], F32).ap()

        def rows(a):
            return a.rearrange("(t p) d -> p t d", p=P)

        x_r, y_r, q_r, v_r, out_r = rows(x), rows(y_dram), rows(q_dram), rows(v_dram), rows(out)

        acc = sb("acc", [P, TILES, D], F32)
        edges = sb("edges", [P, CHUNKS, 2], I32)
        w_split = sb("w_split", [P, 2, 2, KD, D], F32R)
        r_pool = sb("r_pool", [P, 8192], F32R)
        f_pool = sb("f_pool", [P, 7168], F32)
        ident = sb("ident", [P, P], F32)
        iota_row = sb("iota_row", [P, P], F32)
        tables = sb("tables", [P, max(3 * STEPS, 2 * D)], I32)
        tab = tables[0:1, 0:2 * STEPS].rearrange("p (w s) -> p w s", w=2)
        off_t = tables[:, 2 * STEPS:3 * STEPS].bitcast(F32)
        stage = sb("stage", [P, max(RINGS), K, 2], I32)
        var_q = sb("var_q", [P, 64], F32)
        s0 = sb("s0", [P, TILES], F32)
        dinv = sb("dinv", [P, TILES], F32)
        rstd = sb("rstd", [P, TILES], F32)
        cs = sb("cs", [P, TILES, 4], F32)
        cs_split = sb("cs_split", [P, TILES, 2, 2], F32R)
        q_col = sb("q_col", [P, 2, KD], F32)
        small = sb("small", [P, 64], F32)
        dst_rel = sb("dst_rel", [P, 2, K], F32)
        bank = [ctx.enter_context(nc.psum_tensor(f"bank{b}", [P, D], F32)) for b in range(8)]
        agg_bank = bank[6:8]

        g_hl = r_pool[:, 0:4096].rearrange("p (s h f) -> p s h f", s=2, h=2)
        x_hl = r_pool[:, 4096:6144].rearrange("p (s h d) -> p s h d", s=2, h=2)
        biases = r_pool[:, 6144:7168].rearrange("p (w d) -> p w d", w=2)
        ones_row = r_pool[:, 7168:7296]
        onehot = r_pool[:, 7296:7296 + 2 * K * P].rearrange("p (s k n) -> p s k n", s=2, k=K)
        qv_hl = w_split[:, 1, :, :, :].rearrange("p h c d -> p (h c d)").rearrange(
            "p (s w h d) -> p s w h d", s=2, w=2, h=2)
        wg_hl = r_pool[:, 0:4096].rearrange("p (h c d) -> p h c d", h=2, c=KD)
        qz_hl = r_pool[:, 4096:8192].rearrange("p (s w h d) -> p s w h d", s=2, w=2, h=2)
        gath = f_pool[:, 0:max(RINGS) * K * D].rearrange("p (s f) -> p s f", s=max(RINGS))
        x_in = f_pool[:, 5120:5632]
        v_out = f_pool[:, 5632:6144]
        q_out = f_pool[:, 6144:7168].rearrange("p (s d) -> p s d", s=2)
        dist = f_pool[:, 6144:6144 + K * P].rearrange("p (k n) -> p k n", k=K)
        qv_in = f_pool[:, 4096:6144].rearrange("p (s w d) -> p s w d", s=2, w=2)

        def apart(eng):
            eng.nop(nofuse=True)

        def wait(eng, semaphore, value):
            if not (isinstance(value, int) and value <= 0):
                eng.wait_ge(semaphore, value)

        EARLY = 4
        XG = 7
        assert TILES % XG == 0
        spare = acc[:, EARLY * XG:TILES, :].rearrange("p t d -> p (t d)")
        e_rows = spare[:, 0:2 * CHUNKS].bitcast(I32).rearrange("p (a b e) -> p a b e", a=2, b=ROWBLOCKS)
        e_rowsf = spare[:, 2 * CHUNKS:4 * CHUNKS].rearrange("p (a b e) -> p a b e", a=2, b=ROWBLOCKS)
        wv_in = spare[:, 8192:10240].rearrange("p (c d) -> p c d", c=KD)
        wq_in = f_pool[:, 3584:5632].rearrange("p (c d) -> p c d", c=KD)
        b_in = f_pool[:, 5632:6656].rearrange("p (w d) -> p w d", w=2)
        near = f_pool[:, 0:XG * W].bitcast(I32).rearrange("p (s e) -> p s e", s=XG)
        ones = f_pool[:, 6720:6848]
        near_no = f_pool[:, 7160:7160 + XG].bitcast(I32)
        early = tables[:].bitcast(F32)
        ends = early[:, 0:EPAD // W]
        step_down = early[:, 256:256 + P]
        wrap_down = early[:, 384:384 + P]
        from_last = early[:, 512:512 + P]
        full, part, cum, node = (early[:, 640 + 64 * n:640 + 64 * n + TILES] for n in range(4))
        cum_i = f_pool[:, 128:128 + TILES].bitcast(I32)
        met_i = f_pool[:, 192:192 + TILES].bitcast(I32)
        rank = f_pool[:, 256:256 + TILES]
        cmp_t = f_pool[:, 320:320 + TCOLS * (TILES - 1)].rearrange("p (c t) -> p c t", c=TCOLS)
        step_no = f_pool[:, 6848:6848 + TCOLS]
        half = f_pool[:, 6856:6856 + TILES]
        t_f = f_pool[:, 6976:6976 + TCOLS]
        g_f = f_pool[:, 6984:6984 + TCOLS]
        off_f = f_pool[:, 6992:6992 + TCOLS]
        tab_i = f_pool[:, 7000:7000 + 2 * TCOLS].bitcast(I32).rearrange("p (w c) -> p w c", w=2)
        deg = f_pool[:, 7104:7104 + TILES]

        ld_rows, ld_w, ld_b = sem("ld_rows"), sem("ld_w"), sem("ld_b")
        ld_xe, ld_xl = sem("ld_xe"), sem("ld_xl")
        consts, consts_v = sem("consts"), sem("consts_v")
        chain0 = sem("chain0")
        rows_f, rows_t = sem("rows_f"), sem("rows_t")
        ends_spread, ranked, near_ready = sem("ends_spread"), sem("ranked"), sem("near_ready")
        near_got = [sem(f"near_got{u}") for u in range(XG)]
        inside, cum_ready, counted = sem("inside"), sem("cum_ready"), sem("counted")
        deg_ready, dinv_ready, table_ready = sem("deg_ready"), sem("dinv_ready"), sem("table_ready")
        tab_stored, tab_loaded = sem("tab_stored"), sem("tab_loaded")
        acc_act, acc_dve, y_stored = sem("acc_act"), sem("acc_dve"), sem("y_stored")
        w_hi, w_lo, b_hi = sem("w_hi"), sem("w_lo"), sem("b_hi")

        HEAD, TAIL = slice(0, EARLY * XG), slice(EARLY * XG, TILES)

        def own_rows_act(act, tiles):
            for t in tiles:
                if t < HEAD.stop or t % XG < 3:
                    act.activation(acc[:, t, :], acc[:, t, :], ACT.Copy, scale=dinv[:, t:t + 1]).then_inc(acc_act, 1)

        def own_rows_dve(dve, tiles):
            for t in tiles:
                if t >= HEAD.stop and t % XG >= 3:
                    dve.tensor_scalar(acc[:, t, :], acc[:, t, :], dinv[:, t:t + 1], None, ALU.mult).then_inc(acc_dve, 1)

        with nc.Block() as block:
            @block.sync
            def _(sp):
                chunk_rows = lambda a: a.rearrange("(b p e) -> p b e", p=P, e=P)
                sp.dma_start(e_rows[:, 1], chunk_rows(dst)).then_inc(ld_rows, 16)
                sp.dma_start(e_rows[:, 0], chunk_rows(src)).then_inc(ld_rows, 16)
                sp.dma_start(wq_in, Wq.rearrange("(c p) d -> p c d", p=P)).then_inc(ld_w, 16)
                sp.dma_start(wv_in, Wv.rearrange("(c p) d -> p c d", p=P)).then_inc(ld_w, 16)
                for q in (0, 32):
                    for w, b in enumerate((bq, bv)):
                        sp.dma_start(b_in[q:q + 1, w, :], b[None, :]).then_inc(ld_b, 16)

                def store_group(g):
                    if g < EARLY:
                        sp.wait_ge(acc_act, XG * (g + 1))
                    else:
                        sp.wait_ge(acc_act, XG * EARLY + 3 * (g + 1 - EARLY))
                        sp.wait_ge(acc_dve, 4 * (g + 1 - EARLY))
                    sp.dma_start(y_r[:, XG * g:XG * g + XG, :], acc[:, XG * g:XG * g + XG, :]).then_inc(y_stored, 16)

                for g in range(TILES // XG):
                    if g >= 2:
                        sp.wait_ge(inside, XG * (g - 2) + 1)
                    if g == EARLY:
                        sp.wait_ge(w_lo, 2)
                        sp.wait_ge(rows_t, 1)
                    sp.dma_start(acc[:, XG * g:XG * g + XG, :], x_r[:, XG * g:XG * g + XG, :]
                                 ).then_inc(ld_xe if g < EARLY else ld_xl, 16)
                store_group(0)
                sp.wait_ge(inside, TILES)
                for g in range(1, EARLY):
                    if g == EARLY - 1:
                        sp.wait_ge(table_ready, 3)
                        for w in range(2):
                            sp.dma_start(tab_dram[w].rearrange("(p c) -> p c", p=P), tab_i[:, w, :]).then_inc(tab_stored, 16)
                        sp.dma_start(off_dram[0].rearrange("(p c) -> p c", p=P), off_f).then_inc(tab_stored, 16)
                    store_group(g)
                sp.wait_ge(tab_stored, 48)
                sp.dma_start(tab, tab_dram[None, :, 0:STEPS]).then_inc(tab_loaded, 16)
                sp.dma_start(off_t, off_dram[0:1, 0:STEPS].to_broadcast([P, STEPS])).then_inc(tab_loaded, 16)
                for g in range(EARLY, TILES // XG):
                    store_group(g)
                sp.wait_ge(tab_loaded, 32)

            @block.gpsimd
            def _(pool):
                pool.iota(iota_row[:], [[1, P]], base=0, channel_multiplier=0,
                          allow_small_or_imprecise_dtypes=True).then_inc(consts, 1)
                pool.iota(node, [[P, TILES]], base=0, channel_multiplier=1,
                          allow_small_or_imprecise_dtypes=True).then_inc(consts, 1)
                pool.iota(step_no, [[1, TCOLS]], base=0, channel_multiplier=TCOLS,
                          allow_small_or_imprecise_dtypes=True).then_inc(consts, 1)
                pool.memset(ident[:], 0.0).then_inc(consts, 1)
                pool.memset(from_last, 0.0).then_inc(consts, 1)
                pool.memset(wrap_down, 0.0).then_inc(consts, 1)
                pool.wait_ge(consts, 6)
                pool.affine_select(out=ident[:], in_=ident[:], compare_op=ALU.not_equal, fill=1.0, base=0,
                                   pattern=[[-1, P]], channel_multiplier=1).then_inc(consts, 1)
                pool.memset(half, -0.5).then_inc(consts, 1)
                pool.wait_ge(consts, 8)
                pool.affine_select(out=step_down, in_=ident[:], compare_op=ALU.not_equal, fill=-1.0, base=1,
                                   pattern=[[-1, P]], channel_multiplier=1).then_inc(consts, 1)
                pool.affine_select(out=wrap_down, in_=wrap_down, compare_op=ALU.not_equal, fill=-1.0, base=P - 1,
                                   pattern=[[1, P]], channel_multiplier=-1).then_inc(consts, 1)
                pool.affine_select(out=from_last, in_=from_last, compare_op=ALU.not_equal, fill=1.0, base=P - 1,
                                   pattern=[[0, P]], channel_multiplier=-1).then_inc(consts, 1)

                def find(t, u, again):
                    pool.wait_ge(ranked, t + 1)
                    if again:
                        pool.wait_ge(inside, t - XG + 1)
                    apart(pool)
                    pool.tensor_copy(near_no[:, u:u + 1], full[:, bass.ds(t, 1)]).then_inc(near_ready, 1)
                    pool.wait_ge(near_ready, t + 1)
                    apart(pool)
                    pool.indirect_dma_start(near[:, u, :], None, dst.rearrange("(r e) -> r e", e=W),
                                            bass.IndirectOffsetOnAxis(ap=near_no[:, u:u + 1], axis=0)).then_inc(near_got[u], 16)
                for u in range(XG):
                    find(u, u, False)
                for tiles, groups in ((HEAD, (1, EARLY + 1)), (TAIL, (EARLY + 1, TILES // XG))):
                    with pool.Fori(*groups) as r:
                        for u in range(XG):
                            find(r * XG + u, u, True)
                    pool.wait_ge(deg_ready, 1 if tiles is HEAD else 2)
                    pool.tensor_tensor(dinv[:, tiles], deg[:, tiles], half[:, tiles], ALU.pow).then_inc(dinv_ready, 1)

            @block.scalar
            def _(act):
                for w, w_in in enumerate((wq_in, wv_in)):
                    act.wait_ge(ld_w, 32)
                    act.activation(w_split[:, w, 0], w_in, ACT.Copy).then_inc(w_hi, 1)
                act.wait_ge(consts_v, 2)
                act.wait_ge(ld_b, 64)
                act.activation(biases[0:1], b_in[0:1], ACT.Copy).then_inc(b_hi, 1)
                act.activation(biases[32:33], b_in[32:33], ACT.Copy).then_inc(b_hi, 1)
                act.wait_ge(dinv_ready, 1)
                act.wait_ge(ld_xe, 16 * EARLY)
                own_rows_act(act, range(HEAD.stop))
                act.wait_ge(dinv_ready, 2)
                act.wait_ge(ld_xl, 16 * (TILES // XG - EARLY))
                own_rows_act(act, range(TAIL.start, TILES))

            @block.tensor
            def _(pe):
                pe.wait_ge(consts, 7)
                pe.wait_ge(rows_f, 1)
                for b in range(ROWBLOCKS):
                    last = pe.matmul(bank[6 + b // 4][:, (b % 4) * P:(b % 4) * P + P], e_rowsf[:, 1, b, P - 1:P].to_broadcast([P, P]),
                                     ident[:], start=True, stop=True)
                last.then_inc(ends_spread, 1)
                pe.wait_ge(rows_f, 2)
                for a in range(2):
                    for b in range(ROWBLOCKS):
                        last = pe.transpose(bank[2 * a + b // 4][:, (b % 4) * P:(b % 4) * P + P], e_rowsf[:, a, b, :], ident[:])
                last.then_inc(rows_t, 1)
                pe.wait_ge(consts, 11)
                pe.wait_ge(cum_ready, 1)
                pe.matmul(bank[4][:, HEAD], step_down, cum[:, HEAD], start=True, stop=False)
                pe.matmul(bank[4][:, 1:HEAD.stop], wrap_down, cum[:, 0:HEAD.stop - 1], start=False, stop=True).then_inc(counted, 1)
                pe.wait_ge(cum_ready, 2)
                pe.matmul(bank[5][:, TAIL], step_down, cum[:, TAIL], start=True, stop=False)
                pe.matmul(bank[5][:, TAIL], wrap_down, cum[:, TAIL.start - 1:TAIL.stop - 1], start=False, stop=True)
                pe.matmul(bank[5][:, P:P + TILES], from_last, cum, start=True, stop=True).then_inc(counted, 1)

            @block.vector
            def _(dve):
                done = [0]

                def link(i):
                    done[0] += 1
                    i.then_inc(chain0, 1)
                    dve.wait_ge(chain0, done[0])

                link(dve.memset(ones, 1.0))
                link(dve.memset(biases.bitcast(F32), 0.0))
                dve.memset(ones_row.bitcast(F32), 0.0).then_inc(consts_v, 1)
                dve.wait_ge(consts_v, 1)
                dve.tensor_copy(ones_row[0:1], ones[0:1]).then_inc(consts_v, 1)
                link(dve.tensor_copy(ones_row[32:33], ones[32:33]))
                dve.wait_ge(ld_rows, 32)
                dve.tensor_copy(e_rowsf[:, 1], e_rows[:, 1]).then_inc(rows_f, 1)
                dve.tensor_copy(e_rowsf[:, 0], e_rows[:, 0]).then_inc(rows_f, 1)
                dve.wait_ge(ends_spread, 1)
                step = W // P
                link(dve.tensor_copy(ends[:, 0:4 * P // step], bank[6][:, step - 1:4 * P:step]))
                link(dve.tensor_copy(ends[:, 4 * P // step:EPAD // W], bank[7][:, step - 1:CHUNKS - 4 * P:step]))
                dve.wait_ge(consts, 2)

                def rank_nodes(t):
                    wait(dve, ranked, t)
                    dve.tensor_scalar(bank[6][:, 0:EPAD // W], ends, node[:, bass.ds(t, 1)], None, ALU.is_le, ALU.add,
                                      accum_out=full[:, bass.ds(t, 1)]).then_inc(ranked, 1)

                def count_inside(t, r, u):
                    dve.wait_ge(near_got[u], (r + 1) * 16)
                    wait(dve, inside, t)
                    dve.tensor_scalar(bank[7][:], near[:, u], node[:, bass.ds(t, 1)], None, ALU.is_le, ALU.add,
                                      accum_out=part[:, bass.ds(t, 1)]).then_inc(inside, 1)
                for t in range(XG):
                    rank_nodes(t)
                dve.wait_ge(rows_t, 1)
                for a in range(2):
                    to = edges[:, :, a] if a == 0 else edges[:, :, a].bitcast(F32)
                    dve.tensor_copy(to[:, 0:4 * P], bank[2 * a][:]).then_inc(chain0, 1)
                    dve.tensor_copy(to[:, 4 * P:CHUNKS], bank[2 * a + 1][:, 0:CHUNKS - 4 * P]).then_inc(chain0, 1)
                    done[0] += 2
                for u in range(XG):
                    rank_nodes(XG + u)
                    count_inside(u, 0, u)
                for w, w_in in enumerate((wq_in, wv_in)):
                    dve.wait_ge(w_hi, w + 1)
                    dve.tensor_tensor(w_split[:, w, 1], w_in, w_split[:, w, 0].bitcast(F32), ALU.subtract).then_inc(w_lo, 1)

                def degrees(tiles, nth):
                    dve.wait_ge(inside, tiles.stop)
                    dve.scalar_tensor_tensor(cum[:, tiles], full[:, tiles], float(W), part[:, tiles], ALU.mult, ALU.add
                                             ).then_inc(cum_ready, 1)
                    dve.wait_ge(counted, nth)
                    dve.tensor_scalar(deg[:, tiles], bank[3 + nth][:, tiles], 1.0, 1e-12, ALU.add, ALU.max).then_inc(deg_ready, 1)

                for groups in ((1, EARLY), (EARLY, TILES // XG - 1)):
                    with dve.Fori(*groups) as r:
                        for u in range(XG):
                            rank_nodes(r * XG + (XG + u))
                            count_inside(r * XG + u, r, u)
                    if groups[1] == EARLY:
                        degrees(HEAD, 1)
                for u in range(XG):
                    count_inside(TILES - XG + u, TILES // XG - 1, u)
                degrees(TAIL, 2)
                dve.wait_ge(b_hi, 2)
                link(dve.tensor_tensor(biases[32:33], b_in[32:33], biases[32:33].bitcast(F32), ALU.subtract))
                link(dve.tensor_copy(cum_i, bank[5][:, P:P + TILES]))
                link(dve.tensor_scalar(met_i, cum_i, int(math.log2(L)), None, ALU.logical_shift_right))
                link(dve.tensor_copy(rank, met_i))
                link(dve.tensor_tensor(rank[:, 0:TILES - 1], rank[:, 0:TILES - 1], iota_row[:, 1:TILES], ALU.add))
                link(dve.tensor_tensor(cmp_t, rank[:, 0:TILES - 1].unsqueeze(1).to_broadcast([P, TCOLS, TILES - 1]),
                                       step_no.unsqueeze(2).to_broadcast([P, TCOLS, TILES - 1]), ALU.is_le))
                link(dve.tensor_reduce(t_f, cmp_t, AX.X, ALU.add))
                link(dve.tensor_tensor(g_f, step_no, t_f, ALU.subtract))
                dve.tensor_copy(tab_i[:, 0, :], t_f).then_inc(table_ready, 1)
                dve.tensor_copy(tab_i[:, 1, :], g_f).then_inc(table_ready, 1)
                dve.tensor_scalar(off_f, t_f, float(P), None, ALU.mult).then_inc(table_ready, 1)
                dve.wait_ge(dinv_ready, 2)
                dve.wait_ge(ld_xl, 16 * (TILES // XG - EARLY))
                own_rows_dve(dve, range(TAIL.start, TILES))

        col_ready, gathered = sem("col_ready"), [sem(f"gathered{r}") for r in range(max(RINGS))]
        g_hi, g_lo, summed_up, added = sem("g_hi"), sem("g_lo"), sem("summed_up"), sem("added")
        rel_ready, distance, hot_ready = sem("rel_ready"), sem("distance"), sem("hot_ready")

        class Steps:

            def __init__(self, phase):
                self.n = PHASE_STEPS[phase]
                self.base = TILES * sum(PHASE_STEPS[:phase])
                self.ring = RINGS[phase]
                self.act_hot = ACT_HOT[phase]
                self.hots = sum(TILES * n for n, a in zip(PHASE_STEPS[:phase], ACT_HOT) if a)
                assert 2 * self.n % self.ring == 0
                self.uses = [sum(len(range(b, TILES * n, ring)) for n, ring in zip(PHASE_STEPS[:phase], RINGS)
                                 if b < ring) for b in range(max(RINGS))]

            def lows(self, u):
                return (u - self.base) * (1 if self.act_hot else 2) + self.base * 2 - self.hots

            def number(self, off, pair, j):
                c = off * self.n + j
                return self.base + c + pair * (2 * self.n), c

            def value(self, engine, row, s, top):
                _, v = nc.values_load_multi_w_load_instructions(
                    tab[0:1, row, bass.ds(s, 1)], [engine], min_val=0, max_val=top)
                return v[0]

            def pool_turn(self, pool, off, pair):
                first = isinstance(pair, int) and off == 0
                last = isinstance(pair, int) and off == TILES - 1
                if first:
                    self.columns(pool, off, pair, 0)
                for j in range(self.n):
                    u, c = self.number(off, pair, j)
                    slot = c % self.ring
                    if not (last and j == self.n - 1):
                        self.columns(pool, off, pair, j + 1)
                    pool.wait_ge(col_ready, u + 1)
                    apart(pool)
                    for k in range(K):
                        pool.indirect_dma_start(gath[:, slot, k * D:k * D + D], None, y_dram,
                                                bass.IndirectOffsetOnAxis(ap=stage[:, slot, k, 0:1], axis=0)
                                                ).then_inc(gathered[slot], 16)

            def columns(self, pool, off, pair, j):
                u, c = self.number(off, pair, j)
                group = self.value(ENG.Pool, 1, u, CHUNKS // K - 1)
                if not (isinstance(pair, int) and c < self.ring):
                    pool.wait_ge(g_lo, self.lows(u - self.ring + 1))
                    apart(pool)
                pool.tensor_copy(stage[:, c % self.ring], edges[:, bass.ds(group * K, K), :]).then_inc(col_ready, 1)

            def act_step(self, act, off, pair, j):
                u, c = self.number(off, pair, j)
                slot = c % self.ring
                act.wait_ge(gathered[slot], (self.uses[slot] + c // self.ring + 1 + pair * (2 * self.n // self.ring)) * (16 * K))
                if not (isinstance(pair, int) and c < 2):
                    act.wait_ge(summed_up, u - 1)
                act.activation(g_hl[:, c % 2, 0], gath[:, slot], ACT.Copy).then_inc(g_hi, 1)
                if not self.act_hot:
                    return
                h = u - self.base + self.hots
                if isinstance(pair, int) and c == 0:
                    self.distances(act, h, c)
                act.wait_ge(distance, (h + 1) * K)
                act.activation(onehot[:, c % 2], dist, ACT.Relu, bias=1.0, scale=-1.0).then_inc(hot_ready, 1)
                if not (isinstance(pair, int) and c == TILES * self.n - 1):
                    self.distances(act, h + 1, c + 1)

            def distances(self, act, h, c):
                act.wait_ge(rel_ready, h + 1)
                wait(act, hot_ready, h)
                for k in range(K):
                    act.activation(dist[:, k, :], iota_row[:], ACT.Abs, bias=dst_rel[:, c % 2, k:k + 1],
                                   scale=-1.0).then_inc(distance, 1)

            def relative(self, dve, u, c):
                h = u - self.base + self.hots
                dve.wait_ge(col_ready, u + 1)
                wait(dve, distance, (h - 1) * K)
                dve.tensor_scalar(dst_rel[:, c % 2], stage[:, c % self.ring, :, 1].bitcast(F32), off_t[:, bass.ds(u, 1)],
                                  None, ALU.subtract).then_inc(rel_ready, 1)

            def dve_step(self, dve, off, pair, j):
                u, c = self.number(off, pair, j)
                slot = c % self.ring
                if self.act_hot:
                    if isinstance(pair, int) and c == 0:
                        self.relative(dve, u, c)
                    if not (isinstance(pair, int) and c == TILES * self.n - 1):
                        self.relative(dve, u + 1, c + 1)
                else:
                    dve.wait_ge(col_ready, u + 1)
                if not (isinstance(pair, int) and c < 2):
                    dve.wait_ge(summed_up, u - 1)
                if not self.act_hot:
                    dve.scalar_tensor_tensor(onehot[:, c % 2], iota_row[:, None, :].to_broadcast([P, K, P]), off_t[:, bass.ds(u, 1)],
                                             stage[:, slot, :, 1:2].bitcast(F32).to_broadcast([P, K, P]),
                                             ALU.add, ALU.is_equal).then_inc(g_lo, 1)
                dve.wait_ge(g_hi, u + 1)
                dve.tensor_tensor(g_hl[:, c % 2, 1], gath[:, slot], g_hl[:, c % 2, 0].bitcast(F32),
                                  ALU.subtract).then_inc(g_lo, 1)
                if c > 0:
                    self.add(dve, u - 1, (c - 1) % 2)

            def add(self, dve, s, half):
                t = self.value(ENG.DVE, 0, s, TILES - 1)
                dve.wait_ge(summed_up, s + 1)
                if not (isinstance(s, int) and s == 0):
                    dve.wait_ge(added, s)
                dve.tensor_tensor(row_tile(acc, t), row_tile(acc, t), agg_bank[half][:], ALU.add).then_inc(added, 1)

            def dve_last(self, dve):
                s = self.base + TILES * self.n - 1
                self.add(dve, s, (TILES * self.n - 1) % 2)

            def pe_step(self, pe, off, pair, j):
                u, c = self.number(off, pair, j)
                if self.act_hot:
                    pe.wait_ge(hot_ready, u + 1 - self.base + self.hots)
                pe.wait_ge(g_lo, self.lows(u + 1))
                if not (isinstance(pair, int) and c < 2):
                    pe.wait_ge(added, u - 1)
                for k in range(K):
                    for h in range(2):
                        last = pe.matmul(agg_bank[c % 2][:], onehot[:, c % 2, k, :], g_hl[:, c % 2, h, k * D:k * D + D],
                                         start=k == 0 and h == 0,
                                         stop=k == K - 1 and h == 1)
                last.then_inc(summed_up, 1)

        def row_tile(a, i):
            return a[:, bass.ds(i, 1), :].rearrange("p a d -> p (a d)")

        def for_turns_by_pairs(eng, turn, lag):
            for i in range(3):
                turn(i, 0)
            with eng.Fori(1, (TILES - 3) // 2) as r:
                turn(1, r)
                turn(2, r)
            for i in range(TILES - 2, TILES + lag):
                turn(i, 0)

        def treats(off, pair, lag):
            return not isinstance(pair, int) or 0 <= off - lag < TILES

        x_loaded, v_stored = sem("x_loaded"), sem("v_stored")
        x_turned, x_hi, x_lo = sem("x_turned"), sem("x_hi"), sem("x_lo")
        q_mul, v_mul, q_relu, q_stat, q_done, v_done = (
            sem("q_mul"), sem("v_mul"), sem("q_relu"), sem("q_stat"), sem("q_done"), sem("v_done"))
        q_stored = [sem(f"q_stored{b}") for b in range(2)]
        steps1 = Steps(0)
        q_sq, rstd_ready = sem("q_sq"), sem("rstd_ready")
        minus_half = small[:, 18:19]
        RSTD_EARLY = TILES - 3

        def rstd_of(pool, tiles, before):
            pool.tensor_scalar(rstd[:, tiles], var_q[:, tiles], 1.0 / D, EPS_LN, ALU.mult, ALU.add).then_inc(rstd_ready, 1)
            pool.wait_ge(rstd_ready, before + 1)
            pool.tensor_tensor(rstd[:, tiles], rstd[:, tiles], minus_half.to_broadcast([P, tiles.stop - tiles.start]),
                               ALU.pow).then_inc(rstd_ready, 1)

        q_sum = small[:, 14:16]
        neg_mean = small[:, 16:18]

        with nc.Block() as block:
            @block.sync
            def _(sp):
                def turn(off, pair):
                    i, par = off + pair * 2, off % 2
                    if treats(off, pair, 0):
                        wait(sp, x_turned, i)
                        sp.dma_start(x_in, row_tile(x_r, i)).then_inc(x_loaded, 16)
                    if treats(off, pair, 2):
                        sp.wait_ge(v_done, i - 1)
                        sp.dma_start(row_tile(v_r, i - 2), v_out).then_inc(v_stored, 16)
                    if treats(off, pair, 3):
                        sp.wait_ge(q_done, i - 2)
                        sp.dma_start(row_tile(q_r, i - 3), q_out[:, 1 - par]).then_inc(q_stored[1 - par], 16)
                for_turns_by_pairs(sp, turn, 3)
                sp.wait_ge(v_stored, 16 * TILES)
                for b in range(2):
                    sp.wait_ge(q_stored[b], 16 * ((TILES + 1 - b) // 2))

            @block.gpsimd
            def _(pool):
                pool.memset(minus_half, -0.5).then_inc(rstd_ready, 1)
                pool.wait_ge(y_stored, 16 * (TILES // XG))
                for_turns_by_pairs(pool, lambda off, pair: steps1.pool_turn(pool, off, pair), 0)
                pool.wait_ge(q_sq, RSTD_EARLY)
                rstd_of(pool, slice(0, RSTD_EARLY), 1)

            @block.scalar
            def _(act):
                def turn(off, pair):
                    i, par = off + pair * 2, off % 2
                    for j in range(steps1.n):
                        if treats(off, pair, 0):
                            steps1.act_step(act, off, pair, j)
                        if j == 0 and treats(off, pair, 2):
                            act.wait_ge(v_mul, i - 1)
                            wait(act, v_stored, (i - 2) * 16)
                            act.activation(v_out, bank[2][:], ACT.Copy).then_inc(v_done, 1)
                        if j == 2 and treats(off, pair, 2):
                            act.wait_ge(q_stat, i - 1)
                            act.activation(bank[3][:], q_out[:, par], ACT.Square, bias=neg_mean[:, par:par + 1],
                                           accum_out=var_q[:, bass.ds(i - 2, 1)]).then_inc(q_sq, 1)
                            act.wait_ge(q_sq, i - 1)
                            act.activation(q_out[:, par], q_out[:, par], ACT.Relu, bias=neg_mean[:, par:par + 1],
                                           accum_out=s0[:, bass.ds(i - 2, 1)]).then_inc(q_done, 1)
                        if j == 3 and treats(off, pair, 0):
                            act.wait_ge(x_turned, i + 1)
                            wait(act, v_mul, i - 1)
                            act.activation(x_hl[:, par, 0], bank[0][:], ACT.Copy).then_inc(x_hi, 1)
                        if j == 3 and treats(off, pair, 1):
                            act.wait_ge(q_mul, i)
                            b = 1 - par
                            wait(act, q_stored[b], (pair + (off - 1) // 2) * 16)
                            act.activation(q_out[:, b], bank[1][:], ACT.Relu, accum_out=q_sum[:, b:b + 1]).then_inc(q_relu, 1)
                for_turns_by_pairs(act, turn, 2)

            @block.tensor
            def _(pe):
                def project(w, part, par):
                    dest = bank[1 + w]
                    if part == 0:
                        pe.matmul(dest[:], ones_row, biases[:, w, :], start=True, stop=False)
                    for c in range(KD // 2 * part, KD // 2 * (part + 1)):
                        for a, b in ((0, 0), (0, 1), (1, 0)):
                            last = pe.matmul(dest[:], x_hl[:, par, a, c * P:c * P + P], w_split[:, w, b, c, :],
                                             start=False, stop=c == KD - 1 and a == 1)
                    if part == 1:
                        last.then_inc((q_mul, v_mul)[w], 1)

                def turn(off, pair):
                    i, par = off + pair * 2, off % 2
                    for j in range(steps1.n):
                        if treats(off, pair, 0):
                            steps1.pe_step(pe, off, pair, j)
                        if j < 4 and treats(off, pair, 1):
                            if j == 0:
                                pe.wait_ge(x_lo, i)
                                wait(pe, q_relu, i - 1)
                            if j == 2:
                                wait(pe, v_done, i - 1)
                            project(j // 2, j % 2, 1 - par)
                        if j == 1 and treats(off, pair, 0):
                            pe.wait_ge(x_loaded, (i + 1) * 16)
                            wait(pe, x_lo, i)
                            for c in range(KD):
                                last = pe.transpose(bank[0][:, c * P:c * P + P], x_in[:, c * P:c * P + P], ident[:])
                            last.then_inc(x_turned, 1)
                for_turns_by_pairs(pe, turn, 1)

            @block.vector
            def _(dve):
                dve.wait_ge(y_stored, 16 * (TILES // XG))
                def turn(off, pair):
                    i, par = off + pair * 2, off % 2
                    for j in range(steps1.n):
                        if treats(off, pair, 0):
                            steps1.dve_step(dve, off, pair, j)
                        if j == 1 and treats(off, pair, 2):
                            m = i - 2
                            dve.wait_ge(q_relu, m + 1)
                            wait(dve, q_done, m - 1)
                            dve.tensor_scalar(neg_mean[:, par:par + 1], q_sum[:, par:par + 1], -1.0 / D, None, ALU.mult
                                              ).then_inc(q_stat, 1)
                        if j == 3 and treats(off, pair, 0):
                            dve.wait_ge(x_hi, i + 1)
                            wait(dve, v_mul, i - 1)
                            dve.tensor_tensor(x_hl[:, par, 1], bank[0][:], x_hl[:, par, 0].bitcast(F32), ALU.subtract).then_inc(x_lo, 1)
                for_turns_by_pairs(dve, turn, 2)
                steps1.dve_last(dve)

        chain1, extremes, angles, valid_ready = (
            sem("chain1"), sem("extremes"), sem("angles"), sem("valid_ready"))
        sines, cs_ready = sem("sines"), sem("cs_ready")
        scr = f_pool[:, 6400:6400 + 12 * 64].rearrange("p (n t) -> p n t", t=64)
        node_no, valid, rs, h2, hang, turns, r1, r2, r3, sin_in, trig, hmm = (
            scr[:, n, 0:TILES] for n in range(12))
        ext = small[:, 20:22]
        ext_all = small[:, 22:24]
        mfac = small[:, 24:28]
        TWO_PI = 2 * math.pi
        PI_A = 6.28125
        PI_B = float(int((TWO_PI - PI_A) * 2**21) / 2**21)
        PI_C = TWO_PI - PI_A - PI_B
        ROUND = 1.5 * 2**23

        def angles_pool(pool):
            pool.iota(node_no, [[P, TILES]], base=0, channel_multiplier=1,
                      allow_small_or_imprecise_dtypes=True).then_inc(valid_ready, 1)
            rstd_of(pool, slice(RSTD_EARLY, TILES), 3)
            pool.wait_ge(extremes, 1)
            pool.partition_all_reduce(ext_all, ext, P, bass.bass_isa.ReduceOp.max).then_inc(extremes, 1)

        def angles_dve(dve):
            done = [0]

            def link(i):
                done[0] += 1
                i.then_inc(chain1, 1)
                dve.wait_ge(chain1, done[0])

            dve.wait_ge(valid_ready, 1)
            link(dve.tensor_scalar(valid, node_no, float(N), None, ALU.is_lt))
            dve.wait_ge(rstd_ready, 5)
            link(dve.tensor_tensor(rs, rstd[:], s0[:], ALU.mult))
            link(dve.tensor_tensor(h2, rs, rs, ALU.mult))
            link(dve.tensor_tensor(hmm, h2, valid, ALU.mult))
            link(dve.tensor_reduce(ext[:, 0:1], hmm, AX.X, ALU.max))
            link(dve.tensor_scalar(r1, valid, 1.0, -3e38, ALU.subtract, ALU.mult))
            link(dve.tensor_tensor(r2, hmm, r1, ALU.add))
            link(dve.tensor_reduce(r3[:, 0:1], r2, AX.X, ALU.min))
            dve.tensor_scalar(ext[:, 1:2], r3[:, 0:1], -1.0, None, ALU.mult).then_inc(extremes, 1)
            dve.wait_ge(extremes, 2)
            link(dve.tensor_tensor(mfac[:, 0:1], ext_all[:, 0:1], ext_all[:, 1:2], ALU.add))
            link(dve.tensor_scalar(mfac[:, 1:2], mfac[:, 0:1], 4.0, None, ALU.mult))
            link(dve.reciprocal(mfac[:, 2:3], mfac[:, 1:2]))
            link(dve.tensor_scalar(mfac[:, 3:4], mfac[:, 2:3], math.pi, None, ALU.mult))
            link(dve.tensor_scalar(hang, h2, mfac[:, 3:4], None, ALU.mult))
            for f, shift in enumerate((0.25, 0.0)):
                link(dve.tensor_scalar(turns, hang, 1 / TWO_PI, shift, ALU.mult, ALU.add))
                link(dve.tensor_scalar(r1, turns, ROUND, None, ALU.add))
                link(dve.tensor_scalar(turns, r1, -ROUND, None, ALU.add))
                link(dve.scalar_tensor_tensor(r1, turns, -PI_A, hang, ALU.mult, ALU.add))
                link(dve.scalar_tensor_tensor(r2, turns, -PI_B, r1, ALU.mult, ALU.add))
                link(dve.scalar_tensor_tensor(r3, turns, -PI_C, r2, ALU.mult, ALU.add))
                link(dve.tensor_scalar(r1, r3, shift * TWO_PI, math.pi, ALU.add, ALU.min))
                dve.tensor_scalar(sin_in, r1, -math.pi, None, ALU.max).then_inc(angles, 1)
                dve.wait_ge(sines, f + 1)
                link(dve.tensor_tensor(r1, trig, rstd[:], ALU.mult))
                link(dve.tensor_tensor(r2, r1, valid, ALU.mult))
                link(dve.tensor_copy(cs[:, :, 2 * f], r2))
                link(dve.tensor_copy(cs[:, :, 2 * f + 1], r2))
                link(dve.tensor_copy(cs_split[:, :, f, 0], r2))
                link(dve.tensor_tensor(cs_split[:, :, f, 1], r2, cs_split[:, :, f, 0].bitcast(F32), ALU.subtract))
            dve.sem_inc(cs_ready, 1)

        def angles_act(act):
            for f in range(2):
                act.wait_ge(angles, f + 1)
                act.activation(trig, sin_in, ACT.Sin).then_inc(sines, 1)
            act.wait_ge(cs_ready, 1)

        for f in range(2):
            qv_loaded = [sem(f"qv_loaded{f}{b}") for b in range(2)]
            q_hi, v_hi, qv_lo, kv_mul = sem(f"q_hi{f}"), sem(f"v_hi{f}"), sem(f"qv_lo{f}"), sem(f"kv_mul{f}")
            kv_hi, kv_lo = sem(f"kv_hi{f}"), sem(f"kv_lo{f}")
            steps2 = Steps(1 + f)

            with nc.Block() as block:
                @block.sync
                def _(sp, qv_loaded=qv_loaded, qv_lo=qv_lo):
                    def turn(off, pair):
                        i, par = off + pair * 2, off % 2
                        wait(sp, qv_lo, (i - 1) * 2)
                        for w, a in enumerate((q_r, v_r)):
                            sp.dma_start(qv_in[:, par, w], row_tile(a, i)).then_inc(qv_loaded[par], 16)
                    for_turns_by_pairs(sp, turn, 0)

                @block.gpsimd
                def _(pool, f=f, steps2=steps2):
                    if f == 0:
                        angles_pool(pool)
                    for_turns_by_pairs(pool, lambda off, pair: steps2.pool_turn(pool, off, pair), 0)

                @block.scalar
                def _(act, f=f, steps2=steps2, qv_loaded=qv_loaded, q_hi=q_hi, v_hi=v_hi, kv_mul=kv_mul, kv_hi=kv_hi):
                    if f == 0:
                        angles_act(act)

                    def turn(off, pair):
                        i, par = off + pair * 2, off % 2
                        for j in range(steps2.n):
                            steps2.act_step(act, off, pair, j)
                        act.wait_ge(qv_loaded[par], (off // 2 + pair + 1) * 32)
                        wait(act, kv_mul, i - 1)
                        act.activation(qv_hl[:, par, 0, 0], qv_in[:, par, 0], ACT.Copy).then_inc(q_hi, 1)
                        act.activation(qv_hl[:, par, 1, 0], qv_in[:, par, 1], ACT.Copy,
                                       scale=cs[:, bass.ds(i, 1), 2 * f]).then_inc(v_hi, 1)
                    for_turns_by_pairs(act, turn, 0)
                    act.wait_ge(kv_mul, TILES)
                    for c in range(KD):
                        act.activation(w_split[:, f, 0, c, :], bank[c][:], ACT.Copy).then_inc(kv_hi, 1)

                @block.tensor
                def _(pe, f=f, steps2=steps2, qv_lo=qv_lo, kv_mul=kv_mul):
                    def turn(off, pair):
                        i, par = off + pair * 2, off % 2
                        if treats(off, pair, 1):
                            first = isinstance(pair, int) and off == 1
                            pe.wait_ge(qv_lo, i * 2)
                        share = KD // steps2.n if steps2.n < KD else 1
                        for j in range(max(steps2.n, KD)):
                            if j < steps2.n and treats(off, pair, 0):
                                steps2.pe_step(pe, off, pair, j)
                            if not treats(off, pair, 1):
                                continue
                            for c in range(j * share, min(KD, (j + 1) * share)):
                                for a, b in ((0, 0), (0, 1), (1, 0)):
                                    q = qv_hl[:, 1 - par, 0, a, c * P:c * P + P]
                                    pe.matmul(bank[c][:], q, qv_hl[:, 1 - par, 1, b], start=first and a == 0 and b == 0,
                                              stop=True, skip_group_check=True)
                                    if b == 0:
                                        last = pe.matmul(bank[4][:, 2 * c:2 * c + 2], q,
                                                         cs_split[:, bass.ds(i - 1, 1), f, :].rearrange("p a b -> p (a b)"),
                                                         start=first and c == 0 and a == 0, stop=True, skip_group_check=True)
                                if c == KD - 1:
                                    last.then_inc(kv_mul, 1)
                    for_turns_by_pairs(pe, turn, 1)

                @block.vector
                def _(dve, f=f, steps2=steps2, q_hi=q_hi, v_hi=v_hi, qv_lo=qv_lo, kv_mul=kv_mul, kv_hi=kv_hi, kv_lo=kv_lo):
                    if f == 0:
                        angles_dve(dve)

                    def turn(off, pair):
                        i, par = off + pair * 2, off % 2
                        for j in range(steps2.n):
                            steps2.dve_step(dve, off, pair, j)
                        dve.wait_ge(q_hi, i + 1)
                        dve.tensor_tensor(qv_hl[:, par, 0, 1], qv_in[:, par, 0], qv_hl[:, par, 0, 0].bitcast(F32),
                                          ALU.subtract).then_inc(qv_lo, 1)
                        dve.wait_ge(v_hi, i + 1)
                        dve.scalar_tensor_tensor(qv_hl[:, par, 1, 1], qv_in[:, par, 1], cs[:, bass.ds(i, 1), 2 * f],
                                                 qv_hl[:, par, 1, 0].bitcast(F32), ALU.mult, ALU.subtract).then_inc(qv_lo, 1)
                    for_turns_by_pairs(dve, turn, 0)
                    steps2.dve_last(dve)
                    for c in range(KD):
                        dve.wait_ge(kv_hi, c + 1)
                        dve.tensor_tensor(w_split[:, f, 1, c, :], bank[c][:], w_split[:, f, 0, c, :].bitcast(F32),
                                          ALU.subtract).then_inc(kv_lo, 1)
                    dve.tensor_reduce(q_col[:, f], bank[4][:, 0:2 * KD].rearrange("p (c h) -> p c h", h=2), AX.X, ALU.add
                                      ).then_inc(kv_lo, 1)

        x2 = f_pool[:, 0:1024].rearrange("p (s d) -> p s d", s=2)
        q_sums = f_pool[:, 1024:2048].rearrange("p (f d) -> p f d", f=2)
        q2 = f_pool[:, 2048:3072].rearrange("p (s d) -> p s d", s=2)
        v2 = f_pool[:, 3072:4096].rearrange("p (s d) -> p s d", s=2)
        u2 = f_pool[:, 4096:5120].rearrange("p (s d) -> p s d", s=2)
        t4 = f_pool[:, 5120:7168].rearrange("p (s d) -> p s d", s=4)
        wg_in = f_pool[:, 5120:7168].rearrange("p (c d) -> p c d", c=KD)
        affine = edges[:].rearrange("p c w -> p (c w)")[:, 0:3 * D].bitcast(F32).rearrange("p (a d) -> p a d", a=3)
        z2 = tables[:, 0:2 * D].bitcast(F32).rearrange("p (s d) -> p s d", s=2)
        st1 = small[:, 0:32].rearrange("p (s c) -> p s c", s=2)
        st2 = small[:, 32:64].rearrange("p (s c) -> p s c", s=2)
        nrm = var_q[:, 0:32].rearrange("p (s c) -> p s c", s=2)

        expo = var_q[:, 40:41]

        ld3, wg_hi_done, wg_lo_done, expo_ready = sem("ld3"), sem("wg_hi_done"), sem("wg_lo_done"), sem("expo_ready")
        x3_loaded = [sem(f"x3_loaded{b}") for b in range(2)]
        spread, q_sums_ready = sem("spread"), sem("q_sums_ready")
        q3_loaded = [sem(f"q3_loaded{b}") for b in range(2)]
        v3_loaded = [sem(f"v3_loaded{b}") for b in range(2)]
        out_stored = [sem(f"out_stored{b}") for b in range(4)]
        z_made = sem("z_made")
        turned, t_hi, t_lo = sem("turned"), sem("t_hi"), sem("t_lo")
        mul_a, mul_b, mul_c = sem("mul_a"), sem("mul_b"), sem("mul_c")
        vb, norms, u_a, u_sum, stat1, stat2 = (
            sem("vb"), sem("norms"), sem("u_a"), sem("u_sum"), sem("stat1"), sem("stat2"))
        rstd1, rstd2, shift1, shift2 = sem("rstd1"), sem("rstd2"), sem("shift1"), sem("shift2")
        normed, scaled, residual, out_done = sem("normed"), sem("scaled"), sem("residual"), sem("out_done")

        def for_turns(eng, body):
            for i in range(6):
                body(i, i // 4, i % 4)
            with eng.Fori(1, (TILES - 2) // 4) as r:
                for n in range(2, 6):
                    body(r * 4 + n, r + n // 4, n % 4)
            for i in range((TILES - 2) // 4 * 4 + 2, TILES + 3):
                body(i, i // 4, i % 4)

        def has(i, lag):
            return not isinstance(i, int) or 0 <= i - lag < TILES

        def after(eng, i, first, semaphore, value):
            if not (isinstance(i, int) and i < first):
                eng.wait_ge(semaphore, value)

        with nc.Block() as block:
            @block.sync
            def _(sp):
                sp.dma_start(wg_in, Wg.rearrange("(c p) d -> p c d", p=P)).then_inc(ld3, 16)
                for n, b in enumerate((gamma, beta, bg)):
                    sp.dma_start(affine[:, n], b[None, :].to_broadcast([P, D])).then_inc(ld3, 16)

                def turn(i, r, n):
                    if has(i, 0):
                        after(sp, i, 2, turned, i - 1)
                        after(sp, i, 2, norms, i * 6 - 9)
                        sp.dma_start(q2[:, n % 2], row_tile(q_r, i)).then_inc(q3_loaded[n % 2], 16)
                        after(sp, i, 2, u_sum, (i - 1) * 3)
                        sp.dma_start(v2[:, n % 2], row_tile(v_r, i)).then_inc(v3_loaded[n % 2], 16)
                    if has(i, 2):
                        after(sp, i, 4, residual, i - 3)
                        sp.dma_start(x2[:, n % 2], row_tile(x_r, i - 2)).then_inc(x3_loaded[n % 2], 16)
                    if has(i, 4):
                        sp.wait_ge(out_done, i - 3)
                        sp.dma_start(row_tile(out_r, i - 4), t4[:, n]).then_inc(out_stored[n], 16)
                for_turns(sp, turn)
                sp.wait_ge(out_done, TILES)
                sp.dma_start(row_tile(out_r, TILES - 1), t4[:, (TILES - 1) % 4]).then_inc(out_stored[(TILES - 1) % 4], 16)
                for b in range(4):
                    sp.wait_ge(out_stored[b], 16 * len(range(b, TILES, 4)))

            @block.gpsimd
            def _(pool):
                pool.memset(expo, -0.5).then_inc(expo_ready, 1)
                pool.wait_ge(expo_ready, 1)
                pool.wait_ge(ld3, 64)

                def power(i, lag, stat, st, ready):
                    pool.wait_ge(stat, (i - lag + 1) * 2)
                    apart(pool)
                    pool.tensor_scalar(st[:, 8:9], st[:, 7:8], EPS_LN, None, ALU.add).then_inc(ready, 1)
                    pool.wait_ge(ready, (i - lag) * 2 + 1)
                    pool.tensor_tensor(st[:, 8:9], st[:, 8:9], expo, ALU.pow).then_inc(ready, 1)

                def scale_row(i, n):
                    apart(pool)
                    pool.tensor_tensor(z2[:, n % 2], row_tile(acc, i), dinv[:, bass.ds(i, 1)].to_broadcast([P, D]),
                                       ALU.mult).then_inc(z_made, 1)

                scale_row(0, 0)

                def turn(i, r, n):
                    if has(i, -1):
                        after(pool, i, 1, turned, i)
                        scale_row(i + 1, n + 1)
                    if has(i, 0):
                        pool.wait_ge(v3_loaded[n % 2], (r * 2 + n // 2 + 1) * 16)
                        pool.tensor_tensor(v2[:, n % 2], v2[:, n % 2], affine[:, 2], ALU.add).then_inc(vb, 1)
                    if has(i, 3):
                        power(i, 3, stat2, st2[:, (n - 3) % 2], rstd2)
                    if has(i, 2):
                        t = t4[:, (n - 2) % 4]
                        pool.wait_ge(normed, i - 1)
                        pool.tensor_tensor(t, t, affine[:, 0], ALU.mult).then_inc(scaled, 1)
                        pool.wait_ge(scaled, (i - 2) * 2 + 1)
                        pool.tensor_tensor(t, t, affine[:, 1], ALU.add).then_inc(scaled, 1)
                    if has(i, 1):
                        power(i, 1, stat1, st1[:, (n - 1) % 2], rstd1)
                for_turns(pool, turn)

            @block.scalar
            def _(act):
                def turn(i, r, n):
                    if isinstance(i, int) and i == 1:
                        act.wait_ge(ld3, 64)
                        act.activation(wg_hl[:, 0], wg_in, ACT.Copy).then_inc(wg_hi_done, 1)
                    if has(i, 0):
                        act.wait_ge(turned, i + 1)
                        after(act, i, 2, mul_c, i - 1)
                        for w in range(2):
                            act.activation(qz_hl[:, n % 2, w, 0], bank[w][:], ACT.Copy).then_inc(t_hi, 1)
                    if has(i, 2):
                        b = (n - 2) % 4
                        if isinstance(i, int) and i == 2:
                            act.wait_ge(wg_lo_done, 1)
                        act.wait_ge(shift1, i - 1)
                        after(act, i, 6, out_stored[b], (r + (n - 2) // 4) * 16)
                        s = st1[:, n % 2]
                        act.activation(t4[:, b], u2[:, n % 2], ACT.Identity, bias=s[:, 9:10], scale=s[:, 8:9]).then_inc(normed, 1)
                    if has(i, 1):
                        act.wait_ge(mul_a, i)
                        act.wait_ge(norms, i * 6)
                        after(act, i, 3, normed, i - 2)
                        act.activation(u2[:, (n - 1) % 2], bank[2][:], ACT.Copy, scale=nrm[:, (n - 1) % 2, 6:7]).then_inc(u_a, 1)
                    if has(i, 3):
                        act.wait_ge(shift2, i - 2)
                        s = st2[:, (n - 3) % 2]
                        t = t4[:, (n - 3) % 4]
                        act.activation(t, t, ACT.Identity, bias=s[:, 9:10], scale=s[:, 8:9]).then_inc(out_done, 1)
                for_turns(act, turn)

            @block.tensor
            def _(pe):
                def turn(i, r, n):
                    if has(i, 0):
                        pe.wait_ge(q3_loaded[n % 2], (r * 2 + n // 2 + 1) * 16)
                        after(pe, i, 1, t_lo, i * 2)
                        for c in range(KD):
                            pe.transpose(bank[0][:, c * P:c * P + P], q2[:, n % 2, c * P:c * P + P], ident[:])
                        pe.wait_ge(z_made, i + 1)
                        for c in range(KD):
                            last = pe.transpose(bank[1][:, c * P:c * P + P], z2[:, n % 2, c * P:c * P + P], ident[:])
                        last.then_inc(turned, 1)
                    if has(i, 1):
                        pe.wait_ge(t_lo, i * 2)
                        qz = qz_hl[:, (n - 1) % 2]
                        def product(dest, w, weight, mul):
                            for c in range(KD):
                                for a, b in ((0, 0), (0, 1), (1, 0)):
                                    last = pe.matmul(dest[:], qz[:, w, a, c * P:c * P + P], weight(b, c),
                                                     start=c == 0 and a == 0 and b == 0, stop=c == KD - 1 and a == 1)
                            last.then_inc(mul, 1)
                        after(pe, i, 2, u_a, i - 1)
                        product(bank[2], 0, lambda b, c: w_split[:, 0, b, c, :], mul_a)
                        after(pe, i, 2, u_sum, i * 3 - 5)
                        product(bank[3], 0, lambda b, c: w_split[:, 1, b, c, :], mul_b)
                        after(pe, i, 2, u_sum, i * 3 - 4)
                        if isinstance(i, int) and i == 1:
                            pe.wait_ge(wg_lo_done, 1)
                        product(bank[4], 1, lambda b, c: wg_hl[:, b, c, :], mul_c)
                for f in range(2):
                    for c in range(KD):
                        last = pe.matmul(bank[6 + f][:, c * P:c * P + P], q_col[:, f, c:c + 1].to_broadcast([P, P]), ident[:],
                                         start=True, stop=True)
                last.then_inc(spread, 1)
                for_turns(pe, turn)

            @block.vector
            def _(dve):
                def shift(st, rstd_sem, count, ready):
                    dve.wait_ge(rstd_sem, count)
                    dve.scalar_tensor_tensor(st[:, 9:10], st[:, 6:7], -1.0, st[:, 8:9], ALU.mult, ALU.mult).then_inc(ready, 1)

                def stats(st, a, stat, before):
                    dve.bn_stats(st[:, 0:6], a).then_inc(stat, 1)
                    dve.wait_ge(stat, before + 1)
                    apart(dve)
                    dve.bn_aggr(st[:, 6:8], st[:, 0:6]).then_inc(stat, 1)

                def turn(i, r, n):
                    if isinstance(i, int) and i == 1:
                        dve.wait_ge(wg_hi_done, 1)
                        dve.tensor_tensor(wg_hl[:, 1], wg_in, wg_hl[:, 0].bitcast(F32), ALU.subtract).then_inc(wg_lo_done, 1)
                    if isinstance(i, int) and i == 0:
                        dve.wait_ge(spread, 1)
                        for f in range(2):
                            dve.tensor_copy(q_sums[:, f], bank[6 + f][:]).then_inc(q_sums_ready, 1)
                        dve.wait_ge(q_sums_ready, 2)
                    if has(i, 0):
                        for w in range(2):
                            dve.wait_ge(t_hi, i * 2 + w + 1)
                            dve.tensor_tensor(qz_hl[:, n % 2, w, 1], bank[w][:], qz_hl[:, n % 2, w, 0].bitcast(F32),
                                              ALU.subtract).then_inc(t_lo, 1)
                    if has(i, 2):
                        shift(st1[:, n % 2], rstd1, (i - 1) * 2, shift1)
                    if has(i, 0):
                        s = nrm[:, n % 2]
                        dve.tensor_copy(s[:, 8:12], cs[:, bass.ds(i, 1), :].rearrange("p a b -> p (a b)")).then_inc(norms, 1)
                        for f in range(2):
                            dve.wait_ge(norms, i * 6 + f + 1)
                            dve.tensor_tensor_reduce(bank[5][:], q2[:, n % 2], q_sums[:, f],
                                                     1.0, 0.0, ALU.mult, ALU.add, s[:, f:f + 1]).then_inc(norms, 1)
                        dve.wait_ge(norms, i * 6 + 3)
                        dve.tensor_tensor_reduce(s[:, 2:4], s[:, 0:2], s[:, 8:12:2],
                                                 1.0, EPS_NORM, ALU.mult, ALU.add, s[:, 4:5]).then_inc(norms, 1)
                        dve.wait_ge(norms, i * 6 + 4)
                        dve.reciprocal(s[:, 5:6], s[:, 4:5]).then_inc(norms, 1)
                        dve.wait_ge(norms, i * 6 + 5)
                        dve.tensor_scalar(s[:, 6:8], s[:, 8:12:2], s[:, 5:6], None, ALU.mult).then_inc(norms, 1)
                        dve.wait_ge(norms, i * 6 + 6)
                    if has(i, 3):
                        b = (n - 3) % 4
                        dve.wait_ge(scaled, (i - 2) * 2)
                        dve.wait_ge(x3_loaded[(n - 3) % 2], (r * 2 + (n - 3) // 2 + 1) * 16)
                        dve.scalar_tensor_tensor(t4[:, b], t4[:, b], 0.0, x2[:, (n - 3) % 2], ALU.max, ALU.add).then_inc(residual, 1)
                        dve.wait_ge(residual, i - 2)
                        stats(st2[:, (n - 3) % 2], t4[:, b], stat2, (i - 3) * 2)
                    if has(i, 1):
                        s = nrm[:, (n - 1) % 2]
                        u = u2[:, (n - 1) % 2]
                        m = i - 1
                        dve.wait_ge(u_a, i)
                        dve.wait_ge(mul_b, i)
                        dve.scalar_tensor_tensor(u, bank[3][:], s[:, 7:8], u, ALU.mult, ALU.add).then_inc(u_sum, 1)
                        if has(i, 3):
                            shift(st2[:, (n - 3) % 2], rstd2, (i - 2) * 2, shift2)
                        dve.wait_ge(mul_c, i)
                        dve.wait_ge(u_sum, m * 3 + 1)
                        dve.tensor_tensor(u, bank[4][:], u, ALU.add).then_inc(u_sum, 1)
                        dve.wait_ge(vb, i)
                        dve.wait_ge(u_sum, m * 3 + 2)
                        dve.tensor_tensor(u, u, v2[:, (n - 1) % 2], ALU.add).then_inc(u_sum, 1)
                        dve.wait_ge(u_sum, m * 3 + 3)
                        stats(st1[:, (n - 1) % 2], u, stat1, m * 2)
                    elif has(i, 3):
                        shift(st2[:, (n - 3) % 2], rstd2, (i - 2) * 2, shift2)
                for_turns(dve, turn)


def kernel(x, src, dst, L0_gnn_Wq, L0_gnn_bq, L0_gnn_Wv, L0_gnn_bv, L0_gnn_Wg, L0_gnn_bg, L0_gnn_gamma,
           L0_gnn_beta):
    import numpy as np
    import concourse.bacc as bacc
    from concourse.bass_utils import run_bass_kernel_spmd

    xp = np.zeros((NPAD, D), np.float32)
    xp[:N] = np.asarray(x)
    sp = np.zeros(EPAD, np.int32)
    sp[:E] = np.asarray(src)
    dp = np.full(EPAD, NPAD, np.int32)
    dp[:E] = np.asarray(dst)
    arrays = {"x": xp, "src": sp, "dst": dp, "Wq": L0_gnn_Wq, "bq": L0_gnn_bq, "Wv": L0_gnn_Wv, "bv": L0_gnn_bv,
              "Wg": L0_gnn_Wg, "bg": L0_gnn_bg, "gamma": L0_gnn_gamma, "beta": L0_gnn_beta}
    arrays = {f"in_{k}": np.ascontiguousarray(a) for k, a in arrays.items()}
    nc = bacc.Bacc("TRN2", target_bir_lowering=False, num_devices=1)
    aps = {k[3:]: nc.dram_tensor(k, a.shape, mybir.dt.from_np(a.dtype), kind="ExternalInput").ap()
           for k, a in arrays.items()}
    out = nc.dram_tensor("out_0", (NPAD, D), F32, kind="ExternalOutput").ap()
    build(nc, out=out, **aps)
    r = run_bass_kernel_spmd(nc, [arrays], core_ids=[0])
    return r.results[0]["out_0"][:N]
```
